# Optimizing a Trainium2 kernel written in Bass

```python
import numpy as np
import jax
import jax.numpy as jnp

def _softmax(x, axis=-1):
    return jax.nn.softmax(x, axis=axis)

def _gelu(x):
    return jax.nn.gelu(x, approximate=True)

def _silu(x):
    return jax.nn.silu(x)

def _sigmoid(x):
    return jax.nn.sigmoid(x)

def _layernorm(x, axis=-1, eps=1e-05):
    m = jnp.mean(x, axis=axis, keepdims=True)
    v = jnp.var(x, axis=axis, keepdims=True)
    return (x - m) / jnp.sqrt(v + eps)

def _scatter_add(tgt, idx, src, axis=0):
    return tgt.at[idx].add(src)

def _segment_sum(src, seg, n):
    return jax.ops.segment_sum(src, seg, n)
kernel_name = 'mk_hybrid_d1_jaxref_r8_f4bfc9'

def setup_inputs(seed: int=0):
    np.random.seed(seed)
    _w = jnp.asarray

    def _L0_attn_a_setup():
        import jax, jax.numpy as jnp
        import numpy as np
        D_MODEL = 512
        N_HEADS = 32
        HEAD_DIM = D_MODEL // N_HEADS
        CLIP_QKV = 8.0
        ALIBI_BIAS_MAX = 8.0
        LN_EPS = 1e-05

        def _alibi_slopes(n_heads: int, bias_max: float) -> jnp.ndarray:
            next_pow2 = 2 ** int(np.ceil(np.log2(n_heads)))
            m = np.arange(1, next_pow2 + 1, dtype=np.float32) * (bias_max / next_pow2)
            slopes = 1.0 / np.power(2.0, m)
            if next_pow2 != n_heads:
                slopes = np.concatenate([slopes[1::2], slopes[::2]])[:n_heads]
            return jnp.asarray(slopes)

        def _layer_norm(x, w, b):
            mu = jnp.mean(x, axis=-1, keepdims=True)
            var = jnp.mean(jnp.square(x - mu), axis=-1, keepdims=True)
            return (x - mu) * jax.lax.rsqrt(var + LN_EPS) * w + b
        key = jax.random.key(seed)
        ks = jax.random.split(key, 3)
        B, S = (1, 256)
        hidden_states = jax.random.normal(ks[0], (B, S, D_MODEL), dtype=jnp.float32)
        Wqkv = jax.random.normal(ks[1], (3 * D_MODEL, D_MODEL), dtype=jnp.float32) * 0.02
        Wout = jax.random.normal(ks[2], (D_MODEL, D_MODEL), dtype=jnp.float32) * 0.02
        return {'hidden_states': hidden_states, 'Wqkv': Wqkv, 'q_ln_w': jnp.ones((D_MODEL,), jnp.float32), 'q_ln_b': jnp.zeros((D_MODEL,), jnp.float32), 'k_ln_w': jnp.ones((D_MODEL,), jnp.float32), 'k_ln_b': jnp.zeros((D_MODEL,), jnp.float32), 'Wout': Wout}
    _L0_attn_a_in = _L0_attn_a_setup()

    def _L0_attn_b_setup():
        import jax, jax.numpy as jnp
        import numpy as np
        import math
        B, L, D, H = (32, 64, 512, 32)
        HD = D // H
        key = jax.random.key(seed)
        ks = jax.random.split(key, 9)
        s = 1.0 / math.sqrt(D)
        return {'x': jax.random.normal(ks[0], (B, L, D), jnp.float32), 'Wq': jax.random.normal(ks[1], (D, D), jnp.float32) * s, 'bq': jax.random.normal(ks[2], (D,), jnp.float32) * s, 'Wk': jax.random.normal(ks[3], (D, D), jnp.float32) * s, 'bk': jax.random.normal(ks[4], (D,), jnp.float32) * s, 'Wv': jax.random.normal(ks[5], (D, D), jnp.float32) * s, 'bv': jax.random.normal(ks[6], (D,), jnp.float32) * s, 'Wo': jax.random.normal(ks[7], (D, D), jnp.float32) * s, 'bo': jax.random.normal(ks[8], (D,), jnp.float32) * s}
    _L0_attn_b_in = _L0_attn_b_setup()

    def _L0_ffn_setup():
        import jax, jax.numpy as jnp
        import numpy as np
        H = 512
        I = 1376
        R = 32
        NLEV = 16
        Q_ZERO = 7.5
        Q_STEP = 0.005
        LR_SCALE = 0.02

        def _qlinear(x, q, scale, A, Bm):
            w = (q.astype(jnp.float32) - Q_ZERO) * (scale * Q_STEP)[:, None]
            y = jnp.einsum('bsh,oh->bso', x, w)
            return y + LR_SCALE * (x @ A @ Bm)
        key = jax.random.key(seed)
        ks = jax.random.split(key, 13)
        B, S = (2, 256)
        inp = {'x': jax.random.normal(ks[0], (B, S, H), jnp.float32), 'gate_q': jax.random.randint(ks[1], (I, H), 0, NLEV, jnp.int32), 'gate_scale': jax.random.uniform(ks[2], (I,), jnp.float32), 'gate_A': jax.random.normal(ks[3], (H, R), jnp.float32), 'gate_B': jax.random.normal(ks[4], (R, I), jnp.float32), 'up_q': jax.random.randint(ks[5], (I, H), 0, NLEV, jnp.int32), 'up_scale': jax.random.uniform(ks[6], (I,), jnp.float32), 'up_A': jax.random.normal(ks[7], (H, R), jnp.float32), 'up_B': jax.random.normal(ks[8], (R, I), jnp.float32), 'down_q': jax.random.randint(ks[9], (H, I), 0, NLEV, jnp.int32), 'down_scale': jax.random.uniform(ks[10], (H,), jnp.float32), 'down_A': jax.random.normal(ks[11], (I, R), jnp.float32), 'down_B': jax.random.normal(ks[12], (R, H), jnp.float32)}
        return inp
    _L0_ffn_in = _L0_ffn_setup()
    _d = {'L0_attn_a_hidden_states': _L0_attn_a_in['hidden_states'], 'L0_attn_a_Wqkv': _L0_attn_a_in['Wqkv'], 'L0_attn_a_q_ln_w': _L0_attn_a_in['q_ln_w'], 'L0_attn_a_q_ln_b': _L0_attn_a_in['q_ln_b'], 'L0_attn_a_k_ln_w': _L0_attn_a_in['k_ln_w'], 'L0_attn_a_k_ln_b': _L0_attn_a_in['k_ln_b'], 'L0_attn_a_Wout': _L0_attn_a_in['Wout'], 'L0_attn_b_Wq': _L0_attn_b_in['Wq'], 'L0_attn_b_bq': _L0_attn_b_in['bq'], 'L0_attn_b_Wk': _L0_attn_b_in['Wk'], 'L0_attn_b_bk': _L0_attn_b_in['bk'], 'L0_attn_b_Wv': _L0_attn_b_in['Wv'], 'L0_attn_b_bv': _L0_attn_b_in['bv'], 'L0_attn_b_Wo': _L0_attn_b_in['Wo'], 'L0_attn_b_bo': _L0_attn_b_in['bo'], 'L0_ffn_gate_q': _L0_ffn_in['gate_q'], 'L0_ffn_gate_scale': _L0_ffn_in['gate_scale'], 'L0_ffn_gate_A': _L0_ffn_in['gate_A'], 'L0_ffn_gate_B': _L0_ffn_in['gate_B'], 'L0_ffn_up_q': _L0_ffn_in['up_q'], 'L0_ffn_up_scale': _L0_ffn_in['up_scale'], 'L0_ffn_up_A': _L0_ffn_in['up_A'], 'L0_ffn_up_B': _L0_ffn_in['up_B'], 'L0_ffn_down_q': _L0_ffn_in['down_q'], 'L0_ffn_down_scale': _L0_ffn_in['down_scale'], 'L0_ffn_down_A': _L0_ffn_in['down_A'], 'L0_ffn_down_B': _L0_ffn_in['down_B']}
    _x0 = _d['L0_attn_a_hidden_states']
    _d['L0_attn_a_hidden_states'] = jax.random.normal(jax.random.fold_in(jax.random.key(seed), 1), (4, 512, 512), dtype=_x0.dtype)
    del _x0
    return _d

def reference(L0_attn_a_hidden_states, L0_attn_a_Wqkv, L0_attn_a_q_ln_w, L0_attn_a_q_ln_b, L0_attn_a_k_ln_w, L0_attn_a_k_ln_b, L0_attn_a_Wout, L0_attn_b_Wq, L0_attn_b_bq, L0_attn_b_Wk, L0_attn_b_bk, L0_attn_b_Wv, L0_attn_b_bv, L0_attn_b_Wo, L0_attn_b_bo, L0_ffn_gate_q, L0_ffn_gate_scale, L0_ffn_gate_A, L0_ffn_gate_B, L0_ffn_up_q, L0_ffn_up_scale, L0_ffn_up_A, L0_ffn_up_B, L0_ffn_down_q, L0_ffn_down_scale, L0_ffn_down_A, L0_ffn_down_B):

    def _L0_attn_a_ref(hidden_states, Wqkv, q_ln_w, q_ln_b, k_ln_w, k_ln_b, Wout):
        import jax, jax.numpy as jnp
        import numpy as np
        D_MODEL = 512
        N_HEADS = 32
        HEAD_DIM = D_MODEL // N_HEADS
        CLIP_QKV = 8.0
        ALIBI_BIAS_MAX = 8.0
        LN_EPS = 1e-05

        def _alibi_slopes(n_heads: int, bias_max: float) -> jnp.ndarray:
            next_pow2 = 2 ** int(np.ceil(np.log2(n_heads)))
            m = np.arange(1, next_pow2 + 1, dtype=np.float32) * (bias_max / next_pow2)
            slopes = 1.0 / np.power(2.0, m)
            if next_pow2 != n_heads:
                slopes = np.concatenate([slopes[1::2], slopes[::2]])[:n_heads]
            return jnp.asarray(slopes)

        def _layer_norm(x, w, b):
            mu = jnp.mean(x, axis=-1, keepdims=True)
            var = jnp.mean(jnp.square(x - mu), axis=-1, keepdims=True)
            return (x - mu) * jax.lax.rsqrt(var + LN_EPS) * w + b
        B, S, _ = hidden_states.shape
        qkv = jnp.einsum('bsd,ed->bse', hidden_states, Wqkv)
        qkv = jnp.clip(qkv, -CLIP_QKV, CLIP_QKV)
        q, k, v = jnp.split(qkv, [D_MODEL, 2 * D_MODEL], axis=-1)
        q = _layer_norm(q, q_ln_w, q_ln_b)
        k = _layer_norm(k, k_ln_w, k_ln_b)
        q = q.reshape(B, S, N_HEADS, HEAD_DIM)
        k = k.reshape(B, S, N_HEADS, HEAD_DIM)
        v = v.reshape(B, S, N_HEADS, HEAD_DIM)
        scale = HEAD_DIM ** (-0.5)
        scores = jnp.einsum('bqhd,bkhd->bhqk', q, k) * scale
        slopes = _alibi_slopes(N_HEADS, ALIBI_BIAS_MAX)
        pos = jnp.arange(S)
        rel = (pos[None, :] - pos[:, None]).astype(jnp.float32)
        scores = scores + slopes[None, :, None, None] * rel[None, None]
        causal = pos[None, :] <= pos[:, None]
        scores = jnp.where(causal[None, None], scores, jnp.float32(-1e+30))
        probs = jax.nn.softmax(scores, axis=-1)
        out = jnp.einsum('bhqk,bkhd->bqhd', probs, v).reshape(B, S, D_MODEL)
        return jnp.einsum('bsd,ed->bse', out, Wout)

    def _L0_attn_b_ref(x, Wq, bq, Wk, bk, Wv, bv, Wo, bo):
        import jax, jax.numpy as jnp
        import numpy as np
        import math
        B, L, D, H = (32, 64, 512, 32)
        HD = D // H
        b, l, d = x.shape
        h, hd = (H, HD)
        q = (x @ Wq.T + bq).reshape(b, l, h, hd).transpose(0, 2, 1, 3)
        k = (x @ Wk.T + bk).reshape(b, l, h, hd).transpose(0, 2, 1, 3)
        v = (x @ Wv.T + bv).reshape(b, l, h, hd).transpose(0, 2, 1, 3)
        scores = jnp.einsum('bhqd,bhkd->bhqk', q, k) / math.sqrt(hd)
        causal = jnp.tril(jnp.ones((l, l), bool))
        scores = jnp.where(causal, scores, -jnp.inf)
        att = jax.nn.softmax(scores, axis=-1)
        out = jnp.einsum('bhqk,bhkd->bhqd', att, v)
        out = out.transpose(0, 2, 1, 3).reshape(b, l, d)
        return out @ Wo.T + bo

    def _L0_ffn_ref(x, gate_q, gate_scale, gate_A, gate_B, up_q, up_scale, up_A, up_B, down_q, down_scale, down_A, down_B):
        import jax, jax.numpy as jnp
        import numpy as np
        H = 512
        I = 1376
        R = 32
        NLEV = 16
        Q_ZERO = 7.5
        Q_STEP = 0.005
        LR_SCALE = 0.02

        def _qlinear(x, q, scale, A, Bm):
            w = (q.astype(jnp.float32) - Q_ZERO) * (scale * Q_STEP)[:, None]
            y = jnp.einsum('bsh,oh->bso', x, w)
            return y + LR_SCALE * (x @ A @ Bm)
        g = _qlinear(x, gate_q, gate_scale, gate_A, gate_B)
        u = _qlinear(x, up_q, up_scale, up_A, up_B)
        h = jax.nn.silu(g) * u
        return _qlinear(h, down_q, down_scale, down_A, down_B)
    x = L0_attn_a_hidden_states
    x = x + _L0_attn_a_ref(_layernorm(x, axis=-1), L0_attn_a_Wqkv, L0_attn_a_q_ln_w, L0_attn_a_q_ln_b, L0_attn_a_k_ln_w, L0_attn_a_k_ln_b, L0_attn_a_Wout)
    x = x + _L0_ffn_ref(_layernorm(x, axis=-1), L0_ffn_gate_q, L0_ffn_gate_scale, L0_ffn_gate_A, L0_ffn_gate_B, L0_ffn_up_q, L0_ffn_up_scale, L0_ffn_up_A, L0_ffn_up_B, L0_ffn_down_q, L0_ffn_down_scale, L0_ffn_down_A, L0_ffn_down_B)
    x = x + _L0_attn_b_ref(_layernorm(x, axis=-1), L0_attn_b_Wq, L0_attn_b_bq, L0_attn_b_Wk, L0_attn_b_bk, L0_attn_b_Wv, L0_attn_b_bv, L0_attn_b_Wo, L0_attn_b_bo)
    x = x + _L0_ffn_ref(_layernorm(x, axis=-1), L0_ffn_gate_q, L0_ffn_gate_scale, L0_ffn_gate_A, L0_ffn_gate_B, L0_ffn_up_q, L0_ffn_up_scale, L0_ffn_up_A, L0_ffn_up_B, L0_ffn_down_q, L0_ffn_down_scale, L0_ffn_down_A, L0_ffn_down_B)
    return x

_drawn_inputs = setup_inputs


def setup_inputs(seed=0):
    import zlib

    import numpy as np

    out = dict(_drawn_inputs(seed))
    spreads = {'L0_attn_a_q_ln_w': (1.0, 0.584),
     'L0_attn_a_q_ln_b': (0.0, 0.627),
     'L0_attn_a_k_ln_w': (1.0, 0.583),
     'L0_attn_a_k_ln_b': (0.0, 2.0)}
    factors = {'L0_attn_b_Wq': 3.854,
     'L0_attn_b_bq': 8.0,
     'L0_attn_b_Wk': 3.972,
     'L0_attn_b_bk': 64.0,
     'L0_attn_b_Wv': 3.35,
     'L0_attn_b_bv': 8.0,
     'L0_attn_b_Wo': 3.296,
     'L0_attn_b_bo': 23.105}
    for name, (base, spread) in spreads.items():
        noise = np.random.default_rng([zlib.crc32(name.encode()), seed]).standard_normal(out[name].shape)
        drawn = base * np.exp(spread * noise) if base else spread * noise
        out[name] = jnp.asarray(drawn.astype(out[name].dtype))
    for name, factor in factors.items():
        out[name] = (out[name] * factor).astype(out[name].dtype)
    return out
```

```python
from contextlib import ExitStack

import concourse.bass as bass
from concourse import mybir

F32 = mybir.dt.float32
F32R = mybir.dt.float32r
F16 = mybir.dt.float16
BF16 = mybir.dt.bfloat16
I32 = mybir.dt.int32
ALU = mybir.AluOpType
ACT = mybir.ActivationFunctionType
AX = mybir.AxisListType
RMAX = bass.bass_isa.ReduceOp.max

P = 128
B, S, D = 4, 512, 512
H, HD = 32, 16
I_FFN, RANK = 1376, 32
NT = S // P
NK = D // P
NC = -(-I_FFN // P)
IP = NC * P
CLIP = 8.0
EPS = 1e-5
LR_SCALE, Q_ZERO, Q_STEP = 0.02, 7.5, 0.005
X_SCALE = 2048.0
W_TOP = 30000.0
MASKED = -1e32
HPB = 4
UPH = NT
VW = 3 * HD + 1
BIG = 3e38


def program(nc, a, out):
    ctx = ExitStack()
    with ctx:
        def sb(name, shape, dt):
            return ctx.enter_context(nc.sbuf_tensor(name, shape, dt))

        sem_count = [0]

        phase_sems = []

        def sem_all(name):
            return ctx.enter_context(nc.semaphore(name))

        def sem(name):
            sem_count[0] += 1
            phase_sems.append(nc.alloc_semaphore(name=f"{name}_{sem_count[0]}"))
            return phase_sems[-1]

        def end_phase():
            numbers = sorted(s.num for s in phase_sems)
            runs = [[n, n + 1] for n in numbers if n - 1 not in numbers]
            for run in runs:
                while run[1] in numbers:
                    run[1] += 1
            with nc.Block() as block:
                @block.sync
                def _(sp):
                    for first, end in runs:
                        sp.sem_clear(range(first, end))
            for s in phase_sems:
                nc.release_semaphore(s)
            phase_sems.clear()

        bank = [ctx.enter_context(nc.psum_tensor(f"bank{i}", [P, 512], F32)) for i in range(8)]

        x = sb("x", [P, B * NT * D], F32)
        ident = sb("ident", [P, P], F32)
        gu_hi = sb("gu_hi", [P, NK, 2, IP], F16)
        gu_lo = sb("gu_lo", [P, NK, 2, IP], F16)
        w_down = sb("w_down", [P, NC, D], F32)
        c_gu = sb("c_gu", [P, 1], F32)
        small = sb("small", [P, 64], F32)
        gmax, rmax, wsc, c_qkv, c_q = (small[:, i:i + 1] for i in range(5))
        chunk_max = small[:, 8:32]

        def arena(*specs):
            local = ExitStack()
            sem_count[0] += 1
            return local, [local.enter_context(nc.sbuf_tensor(f"{n}_{sem_count[0]}", s, d)) for n, s, d in specs]

        waits_over = sem_all("waits_over")

        def hold(engine, semaphore, value):
            engine.wait_ge(semaphore, value)
            engine.sem_inc(waits_over, 1)

        def rows(w):
            return w.rearrange("(k p) n -> p k n", p=P)

        def bcast(v):
            return v.rearrange("(a n) -> a n", a=1).partition_broadcast(P)

        def prepare():
            local, (q_raw, w_gu, scale_b, a_t, b_lr, q_down, scale_d, ad_t, bd_lr) = arena(
                ("q_raw", [P, 2, I_FFN], I32), ("w_gu", [P, NK, 2, I_FFN], F32), ("scale_b", [P, 2, I_FFN], F32),
                ("a_t", [RANK, 2, D], F32), ("b_lr", [RANK, 2, 512], F32),
                ("q_down", [P, 2, D], I32), ("scale_d", [P, D], F32),
                ("ad_t", [RANK, 2, P], F32), ("bd_lr", [RANK, D], F32))
            loaded = sem("x_loaded")
            small_in = sem("lowrank_loaded")
            q_in = [sem("q_loaded_even"), sem("q_loaded_odd")]
            qd_in = [sem("qd_loaded_even"), sem("qd_loaded_odd")]
            blr_in = sem("b_lr_loaded")
            ad_in = [sem("ad_loaded_even"), sem("ad_loaded_odd")]
            made = sem("identity_zeroed")
            ident_made = sem("identity_made")
            scaled = sem("scales_ready")
            deq = sem("dequantised")
            ab = sem("lowrank_product")
            summed = sem("weights_summed")
            maxed = sem("chunk_max_ready")
            allmax = sem("all_reduced")
            stat = sem("weight_scale_steps")
            hi = sem("weight_hi")
            lo = sem("weight_lo")
            padded = sem("pads_zeroed")
            NQ = 2 * NK
            pieces = [(0, 512), (512, 512), (1024, I_FFN - 1024)]
            ab_units = [(g, p, k) for g in range(2) for p in range(3) for k in range(NK)]

            with nc.Block() as block:
                @block.sync
                def _(sp):
                    sp.dma_start(scale_b[:, 0, :], bcast(a["gate_scale"])).then_inc(small_in, 16)
                    sp.dma_start(scale_b[:, 1, :], bcast(a["up_scale"])).then_inc(small_in, 16)
                    sp.dma_start(scale_d[:], bcast(a["down_scale"])).then_inc(small_in, 16)
                    sp.dma_start(a_t[:, 0, :], a["gate_A_t"]).then_inc(small_in, 16)
                    sp.dma_start(a_t[:, 1, :], a["up_A_t"]).then_inc(small_in, 16)
                    sp.dma_start(bd_lr[:], a["down_B"]).then_inc(small_in, 16)
                    for n in range(NQ):
                        src = rows(a["gate_q_t" if n < NK else "up_q_t"])
                        if n >= 2:
                            sp.wait_ge(deq, n - 1)
                        sp.dma_start(q_raw[:, n % 2, :], src[:, n % NK, :]).then_inc(q_in[n % 2], 16)
                    for n in range(NC):
                        r = min(P, I_FFN - n * P)
                        if n >= 2:
                            sp.wait_ge(deq, NQ + n - 1)
                        sp.dma_start(q_down[0:r, n % 2, :], a["down_q_t"][n * P:n * P + r, :])\
                            .then_inc(qd_in[n % 2], 16)
                    sp.dma_start(x[:].rearrange("p (t d) -> p t d", d=D),
                                 a["x"].rearrange("(t p) d -> p t d", p=P)).then_inc(loaded, 16)
                    sp.wait_ge(loaded, 16)

                @block.gpsimd
                def _(pool):
                    pool.memset(ident[:], 0.0).then_inc(made, 1)
                    pool.wait_ge(made, 1)
                    pool.affine_select(out=ident[:], in_=ident[:], compare_op=ALU.not_equal, fill=1.0, base=0,
                                       pattern=[[-1, P]], channel_multiplier=1).then_inc(ident_made, 1)
                    pool.memset(gu_hi[:, :, :, I_FFN:IP], 0.0).then_inc(padded, 1)
                    pool.memset(gu_lo[:, :, :, I_FFN:IP], 0.0).then_inc(padded, 1)
                    pool.wait_ge(padded, 2)
                    pool.memset(w_down[I_FFN - (NC - 1) * P:P, NC - 1, :], 0.0).then_inc(padded, 1)
                    pool.wait_ge(padded, 3)
                    pool.wait_ge(stat, 1)
                    pool.partition_all_reduce(gmax, rmax, P, RMAX).then_inc(allmax, 1)

                @block.tensor
                def _(pe):
                    pe.wait_ge(small_in, 96)
                    for n, (g, p, k) in enumerate(ab_units):
                        o, w = pieces[p]
                        if k == 0:
                            pe.wait_ge(blr_in, 16 * (3 * g + p + 1))
                        if n >= 8:
                            pe.wait_ge(summed, n - 7)
                        pe.matmul(bank[n % 8][:, 0:w], a_t[:, g, k * P:(k + 1) * P], b_lr[:, (3 * g + p) % 2, 0:w],
                                  start=True, stop=True).then_inc(ab, 1)
                    base = len(ab_units)
                    for n in range(NC):
                        r = min(P, I_FFN - n * P)
                        pe.wait_ge(ad_in[n % 2], 16 * (n // 2 + 1))
                        pe.wait_ge(summed, base + n - 7)
                        pe.matmul(bank[(base + n) % 8][0:r, :], ad_t[:, n % 2, 0:r], bd_lr[:],
                                  start=True, stop=True).then_inc(ab, 1)

                @block.scalar
                def _(act):
                    for g in range(2):
                        for p, (o, w) in enumerate(pieces):
                            n = 3 * g + p
                            if n >= 1:
                                act.wait_ge(blr_in, 16 * n)
                            if n >= 2:
                                act.wait_ge(ab, NK * (n - 1))
                            act.dma_start(b_lr[:, n % 2, 0:w], a["gate_B" if g == 0 else "up_B"][:, o:o + w])\
                                .then_inc(blr_in, 16)
                    for n in range(NC):
                        r = min(P, I_FFN - n * P)
                        if n >= 2:
                            act.wait_ge(ab, len(ab_units) + n - 1)
                        act.dma_start(ad_t[:, n % 2, 0:r], a["down_A_t"][:, n * P:n * P + r])\
                            .then_inc(ad_in[n % 2], 16)
                    act.wait_ge(stat, 5)
                    for k in range(NK):
                        act.activation(gu_hi[:, k, :, 0:I_FFN], w_gu[:, k, :, :], ACT.Copy, scale=wsc)\
                            .then_inc(hi, 1)

                @block.vector
                def _(dve):
                    dve.wait_ge(small_in, 96)
                    dve.tensor_scalar(scale_b[:], scale_b[:], Q_STEP, None, ALU.mult).then_inc(scaled, 1)
                    dve.tensor_scalar(scale_d[:], scale_d[:], Q_STEP, None, ALU.mult).then_inc(scaled, 1)
                    dve.wait_ge(scaled, 2)
                    for n in range(NQ):
                        dve.wait_ge(q_in[n % 2], 16 * (n // 2 + 1))
                        dve.scalar_tensor_tensor(out=w_gu[:, n % NK, n // NK, :], in0=q_raw[:, n % 2, :],
                                                 scalar=-Q_ZERO, in1=scale_b[:, n // NK, :],
                                                 op0=ALU.add, op1=ALU.mult).then_inc(deq, 1)
                    dve.wait_ge(deq, NQ)
                    for n, (g, p, k) in enumerate(ab_units):
                        o, w = pieces[p]
                        dve.wait_ge(ab, n + 1)
                        dve.scalar_tensor_tensor(out=w_gu[:, k, g, o:o + w], in0=bank[n % 8][:, 0:w],
                                                 scalar=LR_SCALE, in1=w_gu[:, k, g, o:o + w],
                                                 op0=ALU.mult, op1=ALU.add).then_inc(summed, 1)
                    base = len(ab_units)
                    for n in range(NC):
                        r = min(P, I_FFN - n * P)
                        dve.wait_ge(qd_in[n % 2], 16 * (n // 2 + 1))
                        dve.scalar_tensor_tensor(out=w_down[0:r, n, :], in0=q_down[0:r, n % 2, :],
                                                 scalar=-Q_ZERO, in1=scale_d[0:r, :],
                                                 op0=ALU.add, op1=ALU.mult).then_inc(deq, 1)
                        dve.wait_ge(deq, NQ + n + 1)
                        dve.wait_ge(ab, base + n + 1)
                        dve.scalar_tensor_tensor(out=w_down[0:r, n, :], in0=bank[(base + n) % 8][0:r, :],
                                                 scalar=LR_SCALE, in1=w_down[0:r, n, :],
                                                 op0=ALU.mult, op1=ALU.add).then_inc(summed, 1)
                    dve.wait_ge(summed, base)
                    for k in range(NK):
                        dve.tensor_reduce(chunk_max[:, k:k + 1], w_gu[:, k, :, :], AX.XY, ALU.max,
                                          apply_absolute_value=True).then_inc(maxed, 1)
                    dve.wait_ge(maxed, NK)
                    weight_scale(dve, NK, c_gu[:], stat, allmax)
                    for k in range(NK):
                        dve.wait_ge(hi, k + 1)
                        dve.scalar_tensor_tensor(out=gu_lo[:, k, :, 0:I_FFN], in0=w_gu[:, k, :, :], scalar=wsc,
                                                 in1=gu_hi[:, k, :, 0:I_FFN], op0=ALU.mult, op1=ALU.subtract)\
                            .then_inc(lo, 1)
                    dve.wait_ge(lo, NK)
                    dve.wait_ge(summed, base + NC)
            local.close()
            end_phase()

        def weight_scale(dve, n, undo, stat, allmax):
            dve.tensor_reduce(rmax, chunk_max[:, 0:n], AX.X, ALU.max).then_inc(stat, 1)
            dve.wait_ge(allmax, 1)
            dve.tensor_scalar(gmax, gmax, 1e-30, None, ALU.max).then_inc(stat, 1)
            dve.wait_ge(stat, 2)
            dve.reciprocal(wsc, gmax).then_inc(stat, 1)
            dve.tensor_scalar(undo, gmax, 1.0 / (W_TOP * X_SCALE), None, ALU.mult).then_inc(stat, 1)
            dve.wait_ge(stat, 4)
            dve.tensor_scalar(wsc, wsc, W_TOP, None, ALU.mult).then_inc(stat, 1)
            dve.wait_ge(stat, 5)

        def prepare_attention(weights, w_out, is_b, masks, broadcasts):
            local, (w_raw,) = arena(("w_raw", [P, NK, 3 * D], F32))
            loaded = sem("qkv_loaded")
            other = sem("other_loaded")
            maxed = sem("qkv_max")
            stat = sem("qkv_scale_steps")
            allmax = sem("qkv_all_reduced")
            hi = sem("qkv_hi_done")
            lo = sem("qkv_lo_done")
            mask_step = sem("mask_step")
            fixed = sem("broadcasts_scaled")
            with nc.Block() as block:
                @block.sync
                def _(sp):
                    for w, o in weights:
                        sp.dma_start(w_raw[:, :, o:o + w.shape[1]], rows(w)).then_inc(loaded, 16)
                    sp.dma_start(wo[:], rows(w_out)).then_inc(other, 16)
                    for dst, src, _ in broadcasts:
                        sp.dma_start(dst, bcast(src)).then_inc(other, 16)
                    sp.wait_ge(other, 16 * (1 + len(broadcasts)))

                @block.gpsimd
                def _(pool):
                    if is_b:
                        pool.memset(masks[:], 0.0).then_inc(mask_step, 1)
                    else:
                        pool.iota(masks[:], pattern=[[1, S]], base=-(S - P), channel_multiplier=-1,
                                  allow_small_or_imprecise_dtypes=True).then_inc(mask_step, 1)
                    pool.wait_ge(mask_step, 1)
                    pool.affine_select(out=masks[:], in_=masks[:], compare_op=ALU.is_ge, fill=MASKED,
                                       base=S - P, pattern=[[-1, S]], channel_multiplier=1).then_inc(mask_step, 1)
                    pool.wait_ge(mask_step, 2)
                    pool.wait_ge(stat, 1)
                    pool.partition_all_reduce(gmax, rmax, P, RMAX).then_inc(allmax, 1)

                @block.scalar
                def _(act):
                    act.wait_ge(stat, 5)
                    for k in range(NK):
                        act.activation(qkv_hi[:, k, :], w_raw[:, k, :], ACT.Copy, scale=wsc).then_inc(hi, 1)

                @block.vector
                def _(dve):
                    dve.wait_ge(loaded, 16 * len(weights))
                    for k in range(NK):
                        dve.tensor_reduce(chunk_max[:, k:k + 1], w_raw[:, k, :], AX.X, ALU.max,
                                          apply_absolute_value=True).then_inc(maxed, 1)
                    dve.wait_ge(maxed, NK)
                    weight_scale(dve, NK, c_qkv, stat, allmax)
                    dve.tensor_scalar(c_q, c_qkv, HD ** -0.5, None, ALU.mult).then_inc(stat, 1)
                    for k in range(NK):
                        dve.wait_ge(hi, k + 1)
                        dve.scalar_tensor_tensor(out=qkv_lo[:, k, :], in0=w_raw[:, k, :], scalar=wsc,
                                                 in1=qkv_hi[:, k, :], op0=ALU.mult, op1=ALU.subtract)\
                            .then_inc(lo, 1)
                    dve.wait_ge(other, 16 * (1 + len(broadcasts)))
                    n = 0
                    for dst, _, factor in broadcasts:
                        if factor != 1.0:
                            dve.tensor_scalar(dst, dst, factor, None, ALU.mult).then_inc(fixed, 1)
                            n += 1
                    dve.wait_ge(fixed, n)
                    dve.wait_ge(lo, NK)
                    dve.wait_ge(stat, 6)
            local.close()
            end_phase()

        class Norm:

            def __init__(self, xn, x_hi, x_lo, stats):
                self.xn, self.x_hi, self.x_lo = xn, x_hi, x_lo
                self.raw = stats[:, 0:24].rearrange("p (i s) -> p i s", s=6)
                self.mv = stats[:, 24:32].rearrange("p (i s) -> p i s", s=2)
                self.std = stats[:, 32:36]
                self.rstd = stats[:, 36:40]
                self.stats = sem("bn_stats")
                self.aggr = sem("bn_aggr")
                self.eps = sem("eps_added")
                self.root = sem("roots")
                self.inv = sem("rstd_ready")
                self.xn_ready = sem("xn_ready")
                self.turned = sem("xn_turned")
                self.hi_done = sem("x_hi_done")
                self.lo_done = sem("x_lo_done")

            def vector(self, dve, b):
                for i in range(NT):
                    dve.bn_stats(self.raw[:, i, :], x[:, bass.ds((b * NT + i) * D, D)]).then_inc(self.stats, 1)
                hold(dve, self.stats, b * NT + NT)
                for i in range(NT):
                    dve.bn_aggr(self.mv[:, i, :], self.raw[:, i, :]).then_inc(self.aggr, 1)
                dve.wait_ge(self.aggr, b * NT + NT)
                dve.tensor_scalar(self.std, self.mv[:, :, 1], EPS, None, ALU.add).then_inc(self.eps, 1)
                dve.wait_ge(self.root, b + 1)
                dve.reciprocal(self.rstd, self.std).then_inc(self.inv, 1)
                dve.wait_ge(self.inv, b + 1)
                for i in range(NT):
                    dve.tensor_scalar(self.xn[:, i, :], x[:, bass.ds((b * NT + i) * D, D)], self.mv[:, i, 0:1],
                                      self.rstd[:, i:i + 1], ALU.subtract, ALU.mult).then_inc(self.xn_ready, 1)
                for k in range(NK):
                    dve.wait_ge(self.hi_done, b * NK + k + 1)
                    dve.scalar_tensor_tensor(out=self.x_lo[:, k, :], in0=bank[k][:], scalar=X_SCALE,
                                             in1=self.x_hi[:, k, :], op0=ALU.mult, op1=ALU.subtract)\
                        .then_inc(self.lo_done, 1)

            def scalar(self, act, b):
                act.wait_ge(self.eps, b + 1)
                act.activation(self.std, self.std, ACT.Sqrt).then_inc(self.root, 1)
                for k in range(NK):
                    act.wait_ge(self.turned, b * NK + k + 1)
                    act.activation(self.x_hi[:, k, :], bank[k][:], ACT.Copy, scale=X_SCALE)\
                        .then_inc(self.hi_done, 1)

            def tensor(self, pe, b):
                pe.wait_ge(self.xn_ready, b * NT + NT)
                for k in range(NK):
                    for i in range(NT):
                        t = pe.transpose(bank[k][:, i * P:(i + 1) * P], self.xn[:, i, k * P:(k + 1) * P], ident[:])
                    t.then_inc(self.turned, 1)

        def attention(is_b, masks, lnw, bias_out):
            GROUPS = H // HPB
            PAIRS = HPB // 2
            UPB = HPB * UPH
            local, (qkv, v_parts, split_q, split_k, q_t, k_t, s_buf, p_hi, p_lo, head_bias, x_hi, x_lo,
                    o_t, stats, pv_sb) = arena(
                ("qk", [P, 2, NT, D], F32), ("v_parts", [P, NT, H, VW], BF16),
                ("split_q", [P, NT, P], F32R), ("split_k", [P, NT, P], F32R),
                ("q_t", [P, 2, S], F32R), ("k_t", [P, 2, S], F32R),
                ("s_buf", [P, 3, S], F32), ("p_hi", [P, 2, S], F16), ("p_lo", [P, 2, S], F16),
                ("head_bias", [P, 2, S], F32), ("x_hi", [P, NK, S], F16), ("x_lo", [P, NK, S], F16),
                ("o_t", [P, NK, P], F32), ("stats", [P, 128], F32),
                ("pv_sb", [P, NT, HD + 2], F32))
            tmp = head_bias
            att = x_hi[:].rearrange("p k s -> p (k s)").bitcast(F32)
            att2 = x_lo[:].rearrange("p k s -> p (k s)").bitcast(F32)
            half = [att.rearrange("p (i d) -> p i d", d=D), att2.rearrange("p (i d) -> p i d", d=D)]
            norm = Norm(qkv[:, 0], x_hi, x_lo, stats)
            neg_max = stats[:, 40:44]
            rsum = stats[:, 44:48]
            q_raw = stats[:, 48:96].rearrange("p (i s) -> p i s", s=6)
            q_mv = stats[:, 96:112].rearrange("p (i s) -> p i s", s=2)
            q_std = stats[:, 112:120]
            q_rstd = stats[:, 120:128]

            proj = sem("projected")
            evac = sem("qkv_bank_read")
            q_fixed = sem("qk_clipped")
            q_stats = sem("qk_bn_stats")
            q_aggr = sem("qk_bn_aggr")
            q_eps = sem("qk_eps")
            q_root = sem("qk_root")
            q_inv = sem("qk_rstd")
            q_norm = sem("qk_normed")
            q_gain = sem("qk_gained")
            q_done = sem("qk_final")
            v_raw = sem("v_raw")
            v_clip = sem("v_clipped")
            v_h = sem("v_high")
            v_r = sem("v_rest")
            v_m = sem("v_middle")
            v_l = sem("v_low")
            ones = sem("ones_set")
            sp_hi = sem("split_hi")
            sp_lo = sem("split_lo")
            bias_ready = sem("head_bias_ready")
            qk_turned = sem("qk_turned")
            q_t_ready = sem("q_t_ready")
            k_t_ready = sem("k_t_ready")
            s_ready = sem("scores_ready")
            s_masked = sem("scores_masked")
            heads_masked = sem("heads_masked")
            p_ready = sem("probs_ready")
            p_turned = sem("probs_turned")
            hi_ready = sem("probs_hi")
            lo_ready = sem("probs_lo")
            pv_done = sem("pv_done")
            pv_head = sem("pv_head")
            pv_sum = sem("pv_summed")
            r_ready = sem("rsum_ready")
            o_ready = sem("head_out")
            o_turned = sem("o_turned")
            o_t_ready = sem("o_t_ready")
            out_ready = sem("out_ready")
            x_added = sem("x_added")
            bo_added = sem("bo_added")

            units = [(h, i) for h in range(HPB) for i in reversed(range(NT))]
            banks_of = [4, 5, 6, 7, 0, 1, 2, 3]

            with nc.Block() as block:
                @block.tensor
                def _(pe):
                    with pe.Fori(0, B) as b:
                        norm.tensor(pe, b)
                        for i in range(NT):
                            for g in range(3):
                                u = 3 * i + g
                                if u == 0:
                                    pe.wait_ge(norm.lo_done, b * NK + NK)
                                if u >= 8:
                                    pe.wait_ge(evac, b * 12 + u - 7)
                                n = 0
                                for k in range(NK):
                                    for xs, ws in ((x_hi, qkv_hi), (x_lo, qkv_hi), (x_hi, qkv_lo)):
                                        t = pe.matmul(bank[banks_of[u % 8]][:], xs[:, k, i * P:(i + 1) * P],
                                                      ws[:, k, g * D:(g + 1) * D], start=(n == 0),
                                                      stop=(n == 3 * NK - 1))
                                        n += 1
                                t.then_inc(proj, 1)
                        pe.wait_ge(evac, b * 12 + 12)
                        hold(pe, v_l, b * NT + NT)
                        with pe.Fori(0, GROUPS) as hg:
                            def turn_pair(pp):
                                pair = (b * GROUPS + hg) * PAIRS + pp
                                pe.wait_ge(sp_lo, 2 * pair + 2)
                                pe.wait_ge(q_t_ready, pair + 1)
                                pe.wait_ge(k_t_ready, pair + 1)
                                for dst, src in ((bank[6], split_q), (bank[7], split_k)):
                                    for i in range(NT):
                                        t = pe.transpose(dst[:, i * P:(i + 1) * P], src[:, i, :].bitcast(F32),
                                                         ident[:])
                                    t.then_inc(qk_turned, 1)

                            def scores(n):
                                h, i = units[n]
                                unit = (b * GROUPS + hg) * UPB + n
                                if n % (2 * UPH) == 0:
                                    pair = (b * GROUPS + hg) * PAIRS + h // 2
                                    pe.wait_ge(q_t_ready, pair + 2)
                                    pe.wait_ge(k_t_ready, pair + 2)
                                if n >= 2:
                                    pe.wait_ge(s_masked, unit - 1)
                                r = 64 * (h % 2)
                                pe.matmul(bank[n % 2][:, 0:(i + 1) * P], q_t[r:r + 64, h // 2, i * P:(i + 1) * P],
                                          k_t[r:r + 64, h // 2, 0:(i + 1) * P], start=True, stop=True)\
                                    .then_inc(s_ready, 1)

                            def turn_probs(n):
                                h, i = units[n]
                                unit = (b * GROUPS + hg) * UPB + n
                                pe.wait_ge(p_ready, unit + 1)
                                if n >= 2:
                                    pe.wait_ge(lo_ready, unit - 1)
                                for j in range(i + 1):
                                    t = pe.transpose(bank[2 + n % 2][:, j * P:(j + 1) * P],
                                                     s_buf[:, n % 3, j * P:(j + 1) * P], ident[:])
                                t.then_inc(p_turned, 1)

                            def values(n):
                                h, i = units[n]
                                unit = (b * GROUPS + hg) * UPB + n
                                head = (b * GROUPS + hg) * HPB + h
                                pe.wait_ge(lo_ready, unit + 1)
                                if n % UPH == 0 and h >= 2:
                                    pe.wait_ge(pv_sum, head - 1)
                                m = 0
                                for j in range(i + 1):
                                    for part in (p_hi, p_lo):
                                        t = pe.matmul(bank[4 + h % 2][:, i * VW:(i + 1) * VW],
                                                      part[:, n % 2, j * P:(j + 1) * P],
                                                      v_parts[:, j, bass.ds(hg * HPB + h, 1), :],
                                                      start=(m == 0), stop=(m == 2 * i + 1))
                                        m += 1
                                t.then_inc(pv_done, 1)

                            for n in range(UPB + 2):
                                if n < UPB:
                                    if n == 0:
                                        for pp in range(PAIRS):
                                            turn_pair(pp)
                                    scores(n)
                                if 1 <= n <= UPB:
                                    turn_probs(n - 1)
                                if n >= 2:
                                    values(n - 2)
                            pe.wait_ge(pv_sum, ((b * GROUPS + hg) + 1) * HPB)
                        pe.wait_ge(o_ready, (b + 1) * H)
                        for i in range(NT):
                            t_idx = b * NT + i
                            if i >= 1:
                                pe.wait_ge(o_t_ready, t_idx)
                            for k in range(NK):
                                t = pe.transpose(bank[0][:, k * P:(k + 1) * P],
                                                 half[i // 2][:, i % 2, k * P:(k + 1) * P], ident[:])
                            t.then_inc(o_turned, 1)
                            pe.wait_ge(o_t_ready, t_idx + 1)
                            if i >= 2:
                                pe.wait_ge(x_added, t_idx - 1)
                            for k in range(NK):
                                t = pe.matmul(bank[1 + i % 2][:], o_t[:, k, :], wo[:, k, :], start=(k == 0),
                                              stop=(k == NK - 1))
                            t.then_inc(out_ready, 1)
                        pe.wait_ge(x_added, b * NT + NT)

                @block.scalar
                def _(act):
                    with act.Fori(0, B) as b:
                        norm.scalar(act, b)
                        for i in range(NT):
                            for g in range(3):
                                u = 3 * i + g
                                src = bank[banks_of[u % 8]][:]
                                if not is_b:
                                    act.wait_ge(proj, b * 12 + u + 1)
                                    if g < 2:
                                        act.activation(qkv[:, g, i, :], src, ACT.Copy, scale=c_qkv)\
                                            .then_inc(evac, 1)
                                    else:
                                        if i >= 1:
                                            act.wait_ge(v_l, b * NT + i)
                                        act.activation(tmp[:, 0, :], src, ACT.Copy, scale=c_qkv)\
                                            .then_inc(evac, 1)
                                if g == 2:
                                    act.wait_ge(v_clip, b * NT + i + 1)
                                    vv = v_parts[:, i, :, :]
                                    act.copy(vv[:, :, 0:HD], tmp[:, 0, :].rearrange("p (h d) -> p h d", d=HD))\
                                        .then_inc(v_h, 1)
                                    act.wait_ge(v_r, b * NT + i + 1)
                                    act.copy(vv[:, :, HD:2 * HD],
                                             tmp[:, 1, :].rearrange("p (h d) -> p h d", d=HD)).then_inc(v_m, 1)
                        if not is_b:
                            act.wait_ge(q_eps, b + 1)
                            act.activation(q_std, q_std, ACT.Sqrt).then_inc(q_root, 1)
                        with act.Fori(0, GROUPS) as hg:
                            def q_copy(pp):
                                pair = (b * GROUPS + hg) * PAIRS + pp
                                act.wait_ge(qk_turned, 2 * pair + 1 + 1)
                                act.copy(q_t[:, pp, :], bank[6][:]).then_inc(q_t_ready, 1)

                            def exps(n):
                                h, i = units[n]
                                unit = (b * GROUPS + hg) * UPB + n
                                act.wait_ge(s_masked, unit + 1)
                                act.activation(s_buf[:, n % 3, 0:(i + 1) * P], s_buf[:, n % 3, 0:(i + 1) * P],
                                               ACT.Exp, bias=neg_max[:, n % 4:n % 4 + 1], scale=-1.0)\
                                    .then_inc(p_ready, 1)

                            def highs(n):
                                h, i = units[n]
                                unit = (b * GROUPS + hg) * UPB + n
                                act.wait_ge(p_turned, unit + 1)
                                if n >= 2:
                                    act.wait_ge(pv_done, unit - 1)
                                act.copy(p_hi[:, n % 2, 0:(i + 1) * P], bank[2 + n % 2][:, 0:(i + 1) * P])\
                                    .then_inc(hi_ready, 1)

                            for pp in range(PAIRS):
                                q_copy(pp)
                            for n in range(UPB + 1):
                                if n < UPB:
                                    exps(n)
                                if n >= 1:
                                    highs(n - 1)
                        for i in range(NT):
                            act.wait_ge(o_turned, b * NT + i + 1)
                            if i >= 1:
                                act.wait_ge(out_ready, b * NT + i)
                            act.copy(o_t[:].rearrange("p k t -> p (k t)"), bank[0][:]).then_inc(o_t_ready, 1)

                @block.vector
                def _(dve):
                    dve.sem_inc(heads_masked, 2)
                    dve.sem_inc(k_t_ready, 1)
                    dve.sem_inc(q_t_ready, 1)
                    dve.sem_inc(qk_turned, 1)
                    with dve.Fori(0, B) as b:
                        norm.vector(dve, b)
                        for i in range(NT):
                            for g in range(3):
                                u = 3 * i + g
                                src = bank[banks_of[u % 8]][:]
                                dst = qkv[:, g, i, :] if g < 2 else tmp[:, 0, :]
                                if is_b:
                                    dve.wait_ge(proj, b * 12 + u + 1)
                                    if g == 2 and i >= 1:
                                        dve.wait_ge(v_l, b * NT + i)
                                    dve.scalar_tensor_tensor(out=dst, in0=src, scalar=c_q if g == 0 else c_qkv,
                                                             in1=lnw[:, g, :], op0=ALU.mult, op1=ALU.add)\
                                        .then_inc(evac, 1)
                                    if g == 2:
                                        dve.wait_ge(evac, b * 12 + u + 1)
                                        dve.tensor_scalar(tmp[:, 0, 0:1], tmp[:, 0, 0:1], 0.0, None, ALU.add)\
                                            .then_inc(v_clip, 1)
                                else:
                                    dve.wait_ge(evac, b * 12 + u + 1)
                                    dve.tensor_scalar(dst, dst, CLIP, -CLIP, ALU.min, ALU.max)\
                                        .then_inc(v_clip if g == 2 else q_fixed, 1)
                                    if g < 2:
                                        dve.wait_ge(q_fixed, b * 8 + 2 * i + g + 1)
                                        dve.bn_stats(q_raw[:, 2 * i + g, :], dst).then_inc(q_stats, 1)
                            vv = v_parts[:, i, :, :]
                            t0 = tmp[:, 0, :].rearrange("p (h d) -> p h d", d=HD)
                            t1 = tmp[:, 1, :].rearrange("p (h d) -> p h d", d=HD)
                            dve.wait_ge(v_h, b * NT + i + 1)
                            dve.tensor_tensor(t1, t0, vv[:, :, 0:HD], ALU.subtract).then_inc(v_r, 1)
                            dve.wait_ge(v_m, b * NT + i + 1)
                            dve.tensor_tensor(vv[:, :, 2 * HD:3 * HD], t1, vv[:, :, HD:2 * HD], ALU.subtract)\
                                .then_inc(v_l, 1)
                        if not is_b:
                            hold(dve, q_stats, b * 8 + 8)
                            for n in range(8):
                                dve.bn_aggr(q_mv[:, n, :], q_raw[:, n, :]).then_inc(q_aggr, 1)
                            dve.wait_ge(q_aggr, b * 8 + 8)
                            dve.tensor_scalar(q_std, q_mv[:, :, 1], EPS, None, ALU.add).then_inc(q_eps, 1)
                            dve.wait_ge(q_root, b + 1)
                            dve.reciprocal(q_rstd, q_std).then_inc(q_inv, 1)
                            dve.wait_ge(q_inv, b + 1)
                            for n in range(8):
                                i, g = n // 2, n % 2
                                dve.tensor_scalar(qkv[:, g, i, :], qkv[:, g, i, :], q_mv[:, n, 0:1],
                                                  q_rstd[:, n:n + 1], ALU.subtract, ALU.mult).then_inc(q_norm, 1)
                            for n in range(8):
                                i, g = n // 2, n % 2
                                dve.wait_ge(q_norm, b * 8 + n + 1)
                                dve.tensor_tensor(qkv[:, g, i, :], qkv[:, g, i, :], lnw[:, g, :], ALU.mult)\
                                    .then_inc(q_gain, 1)
                            for n in range(8):
                                i, g = n // 2, n % 2
                                dve.wait_ge(q_gain, b * 8 + n + 1)
                                dve.tensor_tensor(qkv[:, g, i, :], qkv[:, g, i, :], lnw[:, 2 + g, :], ALU.add)\
                                    .then_inc(q_done, 1)
                        with dve.Fori(0, GROUPS) as hg:
                            def k_copy(pp):
                                pair = (b * GROUPS + hg) * PAIRS + pp
                                dve.wait_ge(qk_turned, 2 * pair + 2 + 1)
                                dve.tensor_copy(k_t[:, pp, :], bank[7][:]).then_inc(k_t_ready, 1)

                            def mask_max(n):
                                h, i = units[n]
                                unit = (b * GROUPS + hg) * UPB + n
                                head = (b * GROUPS + hg) * HPB + h
                                w = (i + 1) * P
                                if not is_b and n % UPH == 0:
                                    dve.wait_ge(bias_ready, head + 1)
                                if n >= 3:
                                    dve.wait_ge(p_turned, unit - 2)
                                hold(dve, s_ready, unit + 1)
                                table = masks[:, S - w:S] if is_b else head_bias[:, h % 2, S - w:S]
                                dve.tensor_tensor_reduce(out=s_buf[:, n % 3, 0:w], in0=bank[n % 2][:, 0:w],
                                                         in1=table, scale=-1.0, scalar=BIG, op0=ALU.add,
                                                         op1=ALU.min, accum_out=neg_max[:, n % 4:n % 4 + 1])\
                                    .then_inc(s_masked, 1)
                                if n % UPH == UPH - 1 and not is_b:
                                    dve.wait_ge(s_masked, unit + 1)
                                    dve.sem_inc(heads_masked, 1)

                            def lows(n):
                                h, i = units[n]
                                unit = (b * GROUPS + hg) * UPB + n
                                w = (i + 1) * P
                                dve.wait_ge(hi_ready, unit + 1)
                                if n >= 2:
                                    dve.wait_ge(pv_done, unit - 1)
                                dve.tensor_tensor(p_lo[:, n % 2, 0:w], bank[2 + n % 2][:, 0:w],
                                                  p_hi[:, n % 2, 0:w], ALU.subtract).then_inc(lo_ready, 1)

                            def head_out(h):
                                head = (b * GROUPS + hg) * HPB + h
                                dve.wait_ge(pv_done, (b * GROUPS + hg) * UPB + (h + 1) * UPH)
                                src = bank[4 + h % 2][:, 0:NT * VW].rearrange("p (i v) -> p i v", v=VW)
                                dve.reciprocal(rsum, src[:, :, 3 * HD]).then_inc(r_ready, 1)
                                parts = src[:, :, 0:3 * HD].rearrange("p i (t c) -> p i c t", t=3)
                                dve.tensor_reduce(pv_sb[:, :, 0:HD], parts, AX.X, ALU.add).then_inc(pv_sum, 1)
                                dve.wait_ge(r_ready, head + 1)
                                dve.wait_ge(pv_sum, head + 1)
                                for m in range(2):
                                    t = dve.tensor_tensor(
                                        half[m][:, :, bass.ds((hg * HPB + h) * HD, HD)], pv_sb[:, 2 * m:2 * m + 2, 0:HD],
                                        rsum[:, 2 * m:2 * m + 2].unsqueeze(2).to_broadcast([P, 2, HD]), ALU.mult)
                                t.then_inc(o_ready, 1)
                                dve.wait_ge(o_ready, head + 1)

                            for pp in range(PAIRS):
                                k_copy(pp)
                            for n in range(UPB + 2):
                                if n < UPB:
                                    mask_max(n)
                                if n >= 2:
                                    lows(n - 2)
                                if n >= 5 and (n - 5) % UPH == 1:
                                    head_out((n - 5) // UPH)
                            head_out(HPB - 1)
                        for i in range(NT):
                            dve.wait_ge(out_ready, b * NT + i + 1)
                            if is_b and i == 0:
                                dve.wait_ge(bo_added, b * NT + NT)
                            xt = x[:, bass.ds((b * NT + i) * D, D)]
                            dve.tensor_tensor(xt, bank[1 + i % 2][:], xt, ALU.add).then_inc(x_added, 1)

                @block.gpsimd
                def _(pool):
                    for i in range(NT):
                        t = pool.memset(v_parts[:, i, :, 3 * HD:VW], 1.0)
                    t.then_inc(ones, 1)
                    pool.wait_ge(ones, 1)
                    with pool.Fori(0, B) as b:
                        if is_b:
                            hold(pool, norm.xn_ready, b * NT + NT)
                            for i in range(NT):
                                xt = x[:, bass.ds((b * NT + i) * D, D)]
                                pool.tensor_tensor(xt, xt, bias_out[:], ALU.add).then_inc(bo_added, 1)
                        with pool.Fori(0, GROUPS) as hg:
                            for pp in range(PAIRS):
                                pair = (b * GROUPS + hg) * PAIRS + pp
                                col = (hg * HPB + 2 * pp) * HD
                                if pp == 0:
                                    if is_b:
                                        pool.wait_ge(evac, b * 12 + 12)
                                    else:
                                        pool.wait_ge(q_done, b * 8 + 8)
                                for g, buf in ((0, split_q), (1, split_k)):
                                    pool.wait_ge(qk_turned, 2 * pair + 1)
                                    parts = buf[:].rearrange("p i (h m d) -> p (i h) m d", h=2, m=4)
                                    src = qkv[:, g, :, bass.ds(col, 2 * HD)].rearrange("p i (h d) -> p i h d", h=2)
                                    v4 = buf[:].rearrange("p i (h m d) -> p i h m d", h=2, m=4)
                                    hs, ls = ((0, 2), (1, 3)) if g == 0 else ((0, 1), (2, 3))
                                    for m in hs:
                                        t = pool.tensor_copy(v4[:, :, :, m, :], src)
                                    t.then_inc(sp_hi, 1)
                                    hold(pool, sp_hi, 2 * pair + g + 1)
                                    for m in ls:
                                        t = pool.tensor_tensor(v4[:, :, :, m, :], src, v4[:, :, :, hs[1], :],
                                                               ALU.subtract)
                                    t.then_inc(sp_lo, 1)
                                if not is_b:
                                    for h in (2 * pp, 2 * pp + 1):
                                        head = (b * GROUPS + hg) * HPB + h
                                        hold(pool, heads_masked, head + 1)
                                        pool.tensor_tensor(
                                            head_bias[:, h % 2, :], masks[:],
                                            lnw[:, 4, bass.ds(hg * HPB + h, 1)].to_broadcast([P, S]), ALU.mult)\
                                            .then_inc(bias_ready, 1)
            local.close()
            end_phase()

        def ffn(last):
            local, (xn, x_hi, x_lo, dn_hi, dn_lo, sig, hid, h_hi, h_lo, stats) = arena(
                ("xn", [P, NT, D], F32), ("fx_hi", [P, NK, S], F16), ("fx_lo", [P, NK, S], F16),
                ("dn_hi", [P, NC, D], F32R), ("dn_lo", [P, NC, D], F32R),
                ("sig", [P, 2, S], F32), ("hid", [P, 2, S], F32),
                ("h_hi", [P, 2, S], F32R), ("h_lo", [P, 2, S], F32R), ("fstats", [P, 48], F32))
            norm = Norm(xn[:], x_hi, x_lo, stats)
            dhi = sem("down_hi")
            dlo = sem("down_lo")
            gate_ready = sem("gate_ready")
            up_ready = sem("up_ready")
            sig_ready = sem("silu_ready")
            hid_ready = sem("hidden_ready")
            hhi = sem("hidden_hi")
            hlo = sem("hidden_lo")
            down = sem("down_used")
            y_done = sem("down_done")
            x_added = sem("ffn_x_added")
            stored = sem("stored")
            out_v = out.rearrange("(t p) d -> p t d", p=P)
            x_v = x[:].rearrange("p (t d) -> p t d", d=D)

            with nc.Block() as block:
                @block.tensor
                def _(pe):
                    def gate_up(b, c, s):
                        done = b * NC + c
                        for g in range(2):
                            n = 0
                            for k in range(NK):
                                for ws, xs in ((gu_hi, x_hi), (gu_hi, x_lo), (gu_lo, x_hi)):
                                    t = pe.matmul(bank[4 + 2 * s + g][:], ws[:, k, g, bass.ds(c * P, P)], xs[:, k, :],
                                                  start=(n == 0), stop=(n == 3 * NK - 1))
                                    n += 1
                            t.then_inc(up_ready if g else gate_ready, 1)

                    def contract(b, c, s, first=False, end=False):
                        pe.wait_ge(hlo, b * NC + c + 1)
                        for i in range(NT):
                            parts = ((h_hi, dn_hi), (h_lo, dn_hi), (h_hi, dn_lo))
                            for m, (hs, ds_) in enumerate(parts):
                                t = pe.matmul(bank[i][:], hs[:, s, i * P:(i + 1) * P], ds_[:, bass.ds(c, 1), :],
                                              start=(first and m == 0), stop=(end and m == 2))
                        t.then_inc(down, 1)

                    pe.wait_ge(dlo, NC)
                    with pe.Fori(0, B) as b:
                        norm.tensor(pe, b)
                        pe.wait_ge(norm.lo_done, b * NK + NK)
                        gate_up(b, 0, 0)
                        gate_up(b, 1, 1)
                        contract(b, 0, 0, first=True)
                        with pe.Fori(0, (NC - 3) // 2) as j:
                            for s in range(2):
                                c = 2 * j + 2 + s
                                pe.wait_ge(hid_ready, b * NC + c - 1)
                                gate_up(b, c, s)
                                contract(b, c - 1, 1 - s)
                        pe.wait_ge(hid_ready, b * NC + NC - 2)
                        gate_up(b, NC - 1, 0)
                        contract(b, NC - 2, 1)
                        contract(b, NC - 1, 0, end=True)
                        pe.wait_ge(x_added, b * NT + NT)

                @block.scalar
                def _(act):
                    for c in range(NC):
                        act.copy(dn_hi[:, c, :], w_down[:, c, :]).then_inc(dhi, 1)

                    def chunk(b, c, s):
                        act.wait_ge(gate_ready, b * NC + c + 1)
                        act.activation(sig[:, s, :], bank[4 + 2 * s][:], ACT.Silu, scale=c_gu[:]).then_inc(sig_ready, 1)

                    def high(b, c, s, free):
                        act.wait_ge(hid_ready, b * NC + c + 1)
                        if free:
                            act.wait_ge(down, b * NC + c - 1)
                        act.copy(h_hi[:, s, :], hid[:, s, :]).then_inc(hhi, 1)

                    with act.Fori(0, B) as b:
                        norm.scalar(act, b)
                        chunk(b, 0, 0)
                        high(b, 0, 0, False)
                        chunk(b, 1, 1)
                        high(b, 1, 1, False)
                        with act.Fori(0, (NC - 3) // 2) as j:
                            for s in range(2):
                                chunk(b, 2 * j + 2 + s, s)
                                high(b, 2 * j + 2 + s, s, True)
                        chunk(b, NC - 1, 0)
                        high(b, NC - 1, 0, True)

                @block.vector
                def _(dve):
                    for c in range(NC):
                        dve.wait_ge(dhi, c + 1)
                        dve.tensor_tensor(dn_lo[:, c, :], w_down[:, c, :], dn_hi[:, c, :].bitcast(F32), ALU.subtract)\
                            .then_inc(dlo, 1)

                    def chunk(b, c, s, free):
                        dve.wait_ge(sig_ready, b * NC + c + 1)
                        dve.wait_ge(up_ready, b * NC + c + 1)
                        dve.scalar_tensor_tensor(out=hid[:, s, :], in0=bank[5 + 2 * s][:], scalar=c_gu[:],
                                                 in1=sig[:, s, :], op0=ALU.mult, op1=ALU.mult)\
                            .then_inc(hid_ready, 1)
                        dve.wait_ge(hhi, b * NC + c + 1)
                        if free:
                            dve.wait_ge(down, b * NC + c - 1)
                        dve.tensor_tensor(h_lo[:, s, :], hid[:, s, :], h_hi[:, s, :].bitcast(F32), ALU.subtract)\
                            .then_inc(hlo, 1)

                    with dve.Fori(0, B) as b:
                        norm.vector(dve, b)
                        chunk(b, 0, 0, False)
                        chunk(b, 1, 1, False)
                        with dve.Fori(0, (NC - 3) // 2) as j:
                            for s in range(2):
                                chunk(b, 2 * j + 2 + s, s, True)
                        chunk(b, NC - 1, 0, True)
                        dve.wait_ge(down, b * NC + NC)
                        for i in range(NT):
                            xt = x[:, bass.ds((b * NT + i) * D, D)]
                            dve.tensor_tensor(xt, bank[i][:], xt, ALU.add).then_inc(x_added, 1)

                if last:
                    @block.sync
                    def _(sp):
                        with sp.Fori(0, B) as b:
                            sp.wait_ge(x_added, b * NT + NT)
                            sp.dma_start(out_v[:, bass.ds(b * NT, NT), :], x_v[:, bass.ds(b * NT, NT), :])\
                                .then_inc(stored, 16)
                        sp.wait_ge(stored, 16 * B)
            local.close()
            end_phase()

        prepare()
        qkv_hi = sb("qkv_hi", [P, NK, 3 * D], F16)
        qkv_lo = sb("qkv_lo", [P, NK, 3 * D], F16)
        wo = sb("wo", [P, NK, D], F32)
        phase = ExitStack()
        masks = phase.enter_context(nc.sbuf_tensor("masks", [P, S], F32))
        lnw = phase.enter_context(nc.sbuf_tensor("lnw", [P, 5, D], F32))
        prepare_attention([(a["Wqkv_t"], 0)], a["Wout_t"], False, masks,
                          [(lnw[:, 0, :], a["q_ln_w"], HD ** -0.5), (lnw[:, 1, :], a["k_ln_w"], 1.0),
                           (lnw[:, 2, :], a["q_ln_b"], HD ** -0.5), (lnw[:, 3, :], a["k_ln_b"], 1.0),
                           (lnw[:, 4, 0:H], a["alibi_slopes"], 1.0)])
        attention(False, masks, lnw, None)
        phase.close()
        ffn(False)
        phase = ExitStack()
        masks = phase.enter_context(nc.sbuf_tensor("masks_b", [P, S], F32))
        biases = phase.enter_context(nc.sbuf_tensor("biases", [P, 3, D], F32))
        bias_out = phase.enter_context(nc.sbuf_tensor("bias_out", [P, D], F32))
        prepare_attention([(a["Wq_t"], 0), (a["Wk_t"], D), (a["Wv_t"], 2 * D)], a["Wo_t"], True, masks,
                          [(biases[:, 0, :], a["bq"], HD ** -0.5), (biases[:, 1, :], a["bk"], 1.0),
                           (biases[:, 2, :], a["bv"], 1.0), (bias_out[:], a["bo"], 1.0)])
        attention(True, masks, biases, bias_out)
        phase.close()
        ffn(True)


def kernel(**inputs):
    import numpy as np
    import concourse.bacc as bacc
    from concourse.bass_utils import run_bass_kernel_spmd

    def get(name):
        return np.asarray(inputs[name])

    def turned(name):
        return np.ascontiguousarray(get(name).T)

    x = get("L0_attn_a_hidden_states")
    arrays = {
        "x": np.ascontiguousarray(x.reshape(-1, x.shape[-1])),
        "Wqkv_t": turned("L0_attn_a_Wqkv"),
        "Wout_t": turned("L0_attn_a_Wout"),
        "Wq_t": turned("L0_attn_b_Wq"),
        "Wk_t": turned("L0_attn_b_Wk"),
        "Wv_t": turned("L0_attn_b_Wv"),
        "Wo_t": turned("L0_attn_b_Wo"),
        "gate_q_t": turned("L0_ffn_gate_q"),
        "up_q_t": turned("L0_ffn_up_q"),
        "down_q_t": turned("L0_ffn_down_q"),
        "gate_A_t": turned("L0_ffn_gate_A"),
        "up_A_t": turned("L0_ffn_up_A"),
        "down_A_t": turned("L0_ffn_down_A"),
    }
    for name in ("q_ln_w", "q_ln_b", "k_ln_w", "k_ln_b"):
        arrays[name] = get(f"L0_attn_a_{name}")
    for name in ("bq", "bk", "bv", "bo"):
        arrays[name] = get(f"L0_attn_b_{name}")
    for name in ("gate_scale", "gate_B", "up_scale", "up_B", "down_scale", "down_B"):
        arrays[name] = get(f"L0_ffn_{name}")
    arrays["alibi_slopes"] = (1.0 / np.power(2.0, np.arange(1, H + 1, dtype=np.float32) * np.float32(8.0 / H)))\
        .astype(np.float32)

    nc = bacc.Bacc("TRN2", target_bir_lowering=False, num_devices=1)
    args = {name: nc.dram_tensor(f"in_{name}", v.shape, mybir.dt.from_np(v.dtype), kind="ExternalInput").ap()
            for name, v in arrays.items()}
    out = nc.dram_tensor("out_0", (B * S, D), F32, kind="ExternalOutput").ap()
    program(nc, args, out)
    r = run_bass_kernel_spmd(nc, [{f"in_{n}": v for n, v in arrays.items()}], core_ids=[0])
    return r.results[0]["out_0"].reshape(x.shape)
```

```python
from contextlib import ExitStack

import concourse.bass as bass
from concourse import mybir

F32 = mybir.dt.float32
F32R = mybir.dt.float32r
F16 = mybir.dt.float16
BF16 = mybir.dt.bfloat16
I32 = mybir.dt.int32
ALU = mybir.AluOpType
ACT = mybir.ActivationFunctionType
AX = mybir.AxisListType
RMAX = bass.bass_isa.ReduceOp.max

P = 128
B, S, D = 4, 512, 512
H, HD = 32, 16
I_FFN, RANK = 1376, 32
NT = S // P
NK = D // P
NC = -(-I_FFN // P)
IP = NC * P
CLIP = 8.0
EPS = 1e-5
LR_SCALE, Q_ZERO, Q_STEP = 0.02, 7.5, 0.005
X_SCALE = 2048.0
W_TOP = 30000.0
MASKED = -1e32
HPB = 4
UPH = NT
VW = 3 * HD + 1
BIG = 3e38


def program(nc, a, out):
    ctx = ExitStack()
    with ctx:
        def sb(name, shape, dt):
            return ctx.enter_context(nc.sbuf_tensor(name, shape, dt))

        sem_count = [0]

        phase_sems = []

        def sem_all(name):
            return ctx.enter_context(nc.semaphore(name))

        def sem(name):
            sem_count[0] += 1
            phase_sems.append(nc.alloc_semaphore(name=f"{name}_{sem_count[0]}"))
            return phase_sems[-1]

        def end_phase():
            numbers = sorted(s.num for s in phase_sems)
            runs = [[n, n + 1] for n in numbers if n - 1 not in numbers]
            for run in runs:
                while run[1] in numbers:
                    run[1] += 1
            with nc.Block() as block:
                @block.sync
                def _(sp):
                    for first, end in runs:
                        sp.sem_clear(range(first, end))
            for s in phase_sems:
                nc.release_semaphore(s)
            phase_sems.clear()

        bank = [ctx.enter_context(nc.psum_tensor(f"bank{i}", [P, 512], F32)) for i in range(8)]

        x = sb("x", [P, B * NT * D], F32)
        ident = sb("ident", [P, P], F32)
        gu_hi = sb("gu_hi", [P, NK, 2, IP], F16)
        gu_lo = sb("gu_lo", [P, NK, 2, IP], F16)
        w_down = sb("w_down", [P, NC, D], F32)
        minus_half = sb("minus_half", [P, 2 * NT], F32)
        c_gu = sb("c_gu", [P, 1], F32)
        small = sb("small", [P, 64], F32)
        gmax, rmax, wsc, c_qkv, c_q = (small[:, i:i + 1] for i in range(5))
        chunk_max = small[:, 8:32]

        def arena(*specs):
            local = ExitStack()
            sem_count[0] += 1
            return local, [local.enter_context(nc.sbuf_tensor(f"{n}_{sem_count[0]}", s, d)) for n, s, d in specs]

        waits_over = sem_all("waits_over")

        def hold(engine, semaphore, value):
            engine.wait_ge(semaphore, value)
            engine.sem_inc(waits_over, 1)

        def rows(w):
            return w.rearrange("(k p) n -> p k n", p=P)

        def bcast(v):
            return v.rearrange("(a n) -> a n", a=1).partition_broadcast(P)

        def prepare():
            local, (q_raw, w_gu, scale_b, a_t, b_lr, q_down, scale_d, ad_t, bd_lr) = arena(
                ("q_raw", [P, 2, I_FFN], I32), ("w_gu", [P, NK, 2, I_FFN], F32), ("scale_b", [P, 2, I_FFN], F32),
                ("a_t", [RANK, 2, D], F32), ("b_lr", [RANK, 2, 512], F32),
                ("q_down", [P, 2, D], I32), ("scale_d", [P, D], F32),
                ("ad_t", [RANK, 2, P], F32), ("bd_lr", [RANK, D], F32))
            loaded = sem("x_loaded")
            small_in = sem("lowrank_loaded")
            q_in = [sem("q_loaded_even"), sem("q_loaded_odd")]
            qd_in = [sem("qd_loaded_even"), sem("qd_loaded_odd")]
            blr_in = sem("b_lr_loaded")
            ad_in = [sem("ad_loaded_even"), sem("ad_loaded_odd")]
            made = sem("identity_zeroed")
            ident_made = sem("identity_made")
            scaled = sem("scales_ready")
            deq = sem("dequantised")
            ab = sem("lowrank_product")
            summed = sem("weights_summed")
            maxed = sem("chunk_max_ready")
            allmax = sem("all_reduced")
            stat = sem("weight_scale_steps")
            hi = sem("weight_hi")
            lo = sem("weight_lo")
            padded = sem("pads_zeroed")
            NQ = 2 * NK
            pieces = [(0, 512), (512, 512), (1024, I_FFN - 1024)]
            ab_units = [(g, p, k) for g in range(2) for p in range(3) for k in range(NK)]

            with nc.Block() as block:
                @block.sync
                def _(sp):
                    sp.dma_start(scale_b[:, 0, :], bcast(a["gate_scale"])).then_inc(small_in, 16)
                    sp.dma_start(scale_b[:, 1, :], bcast(a["up_scale"])).then_inc(small_in, 16)
                    sp.dma_start(scale_d[:], bcast(a["down_scale"])).then_inc(small_in, 16)
                    sp.dma_start(a_t[:, 0, :], a["gate_A_t"]).then_inc(small_in, 16)
                    sp.dma_start(a_t[:, 1, :], a["up_A_t"]).then_inc(small_in, 16)
                    sp.dma_start(bd_lr[:], a["down_B"]).then_inc(small_in, 16)
                    for n in range(NQ):
                        src = rows(a["gate_q_t" if n < NK else "up_q_t"])
                        if n >= 2:
                            sp.wait_ge(deq, n - 1)
                        sp.dma_start(q_raw[:, n % 2, :], src[:, n % NK, :]).then_inc(q_in[n % 2], 16)
                    for n in range(NC):
                        r = min(P, I_FFN - n * P)
                        if n >= 2:
                            sp.wait_ge(deq, NQ + n - 1)
                        sp.dma_start(q_down[0:r, n % 2, :], a["down_q_t"][n * P:n * P + r, :])\
                            .then_inc(qd_in[n % 2], 16)
                    sp.dma_start(x[:].rearrange("p (t d) -> p t d", d=D),
                                 a["x"].rearrange("(t p) d -> p t d", p=P)).then_inc(loaded, 16)
                    sp.wait_ge(loaded, 16)

                @block.gpsimd
                def _(pool):
                    pool.memset(minus_half[:], -0.5)
                    pool.memset(ident[:], 0.0).then_inc(made, 1)
                    pool.wait_ge(made, 1)
                    pool.affine_select(out=ident[:], in_=ident[:], compare_op=ALU.not_equal, fill=1.0, base=0,
                                       pattern=[[-1, P]], channel_multiplier=1).then_inc(ident_made, 1)
                    pool.memset(gu_hi[:, :, :, I_FFN:IP], 0.0).then_inc(padded, 1)
                    pool.memset(gu_lo[:, :, :, I_FFN:IP], 0.0).then_inc(padded, 1)
                    pool.wait_ge(padded, 2)
                    pool.memset(w_down[I_FFN - (NC - 1) * P:P, NC - 1, :], 0.0).then_inc(padded, 1)
                    pool.wait_ge(padded, 3)
                    pool.wait_ge(stat, 1)
                    pool.partition_all_reduce(gmax, rmax, P, RMAX).then_inc(allmax, 1)

                @block.tensor
                def _(pe):
                    pe.wait_ge(small_in, 96)
                    for n, (g, p, k) in enumerate(ab_units):
                        o, w = pieces[p]
                        if k == 0:
                            pe.wait_ge(blr_in, 16 * (3 * g + p + 1))
                        if n >= 8:
                            pe.wait_ge(summed, n - 7)
                        pe.matmul(bank[n % 8][:, 0:w], a_t[:, g, k * P:(k + 1) * P], b_lr[:, (3 * g + p) % 2, 0:w],
                                  start=True, stop=True).then_inc(ab, 1)
                    base = len(ab_units)
                    for n in range(NC):
                        r = min(P, I_FFN - n * P)
                        pe.wait_ge(ad_in[n % 2], 16 * (n // 2 + 1))
                        pe.wait_ge(summed, base + n - 7)
                        pe.matmul(bank[(base + n) % 8][0:r, :], ad_t[:, n % 2, 0:r], bd_lr[:],
                                  start=True, stop=True).then_inc(ab, 1)

                @block.scalar
                def _(act):
                    for g in range(2):
                        for p, (o, w) in enumerate(pieces):
                            n = 3 * g + p
                            if n >= 1:
                                act.wait_ge(blr_in, 16 * n)
                            if n >= 2:
                                act.wait_ge(ab, NK * (n - 1))
                            act.dma_start(b_lr[:, n % 2, 0:w], a["gate_B" if g == 0 else "up_B"][:, o:o + w])\
                                .then_inc(blr_in, 16)
                    for n in range(NC):
                        r = min(P, I_FFN - n * P)
                        if n >= 2:
                            act.wait_ge(ab, len(ab_units) + n - 1)
                        act.dma_start(ad_t[:, n % 2, 0:r], a["down_A_t"][:, n * P:n * P + r])\
                            .then_inc(ad_in[n % 2], 16)
                    act.wait_ge(stat, 5)
                    for k in range(NK):
                        act.activation(gu_hi[:, k, :, 0:I_FFN], w_gu[:, k, :, :], ACT.Copy, scale=wsc)\
                            .then_inc(hi, 1)

                @block.vector
                def _(dve):
                    dve.wait_ge(small_in, 96)
                    dve.tensor_scalar(scale_b[:], scale_b[:], Q_STEP, None, ALU.mult).then_inc(scaled, 1)
                    dve.tensor_scalar(scale_d[:], scale_d[:], Q_STEP, None, ALU.mult).then_inc(scaled, 1)
                    dve.wait_ge(scaled, 2)
                    for n in range(NQ):
                        dve.wait_ge(q_in[n % 2], 16 * (n // 2 + 1))
                        dve.scalar_tensor_tensor(out=w_gu[:, n % NK, n // NK, :], in0=q_raw[:, n % 2, :],
                                                 scalar=-Q_ZERO, in1=scale_b[:, n // NK, :],
                                                 op0=ALU.add, op1=ALU.mult).then_inc(deq, 1)
                    dve.wait_ge(deq, NQ)
                    for n, (g, p, k) in enumerate(ab_units):
                        o, w = pieces[p]
                        dve.wait_ge(ab, n + 1)
                        dve.scalar_tensor_tensor(out=w_gu[:, k, g, o:o + w], in0=bank[n % 8][:, 0:w],
                                                 scalar=LR_SCALE, in1=w_gu[:, k, g, o:o + w],
                                                 op0=ALU.mult, op1=ALU.add).then_inc(summed, 1)
                    base = len(ab_units)
                    for n in range(NC):
                        r = min(P, I_FFN - n * P)
                        dve.wait_ge(qd_in[n % 2], 16 * (n // 2 + 1))
                        dve.scalar_tensor_tensor(out=w_down[0:r, n, :], in0=q_down[0:r, n % 2, :],
                                                 scalar=-Q_ZERO, in1=scale_d[0:r, :],
                                                 op0=ALU.add, op1=ALU.mult).then_inc(deq, 1)
                        dve.wait_ge(deq, NQ + n + 1)
                        dve.wait_ge(ab, base + n + 1)
                        dve.scalar_tensor_tensor(out=w_down[0:r, n, :], in0=bank[(base + n) % 8][0:r, :],
                                                 scalar=LR_SCALE, in1=w_down[0:r, n, :],
                                                 op0=ALU.mult, op1=ALU.add).then_inc(summed, 1)
                    dve.wait_ge(summed, base)
                    for k in range(NK):
                        dve.tensor_reduce(chunk_max[:, k:k + 1], w_gu[:, k, :, :], AX.XY, ALU.max,
                                          apply_absolute_value=True).then_inc(maxed, 1)
                    dve.wait_ge(maxed, NK)
                    weight_scale(dve, NK, c_gu[:], stat, allmax)
                    for k in range(NK):
                        dve.wait_ge(hi, k + 1)
                        dve.scalar_tensor_tensor(out=gu_lo[:, k, :, 0:I_FFN], in0=w_gu[:, k, :, :], scalar=wsc,
                                                 in1=gu_hi[:, k, :, 0:I_FFN], op0=ALU.mult, op1=ALU.subtract)\
                            .then_inc(lo, 1)
                    dve.wait_ge(lo, NK)
                    dve.wait_ge(summed, base + NC)
            local.close()
            end_phase()

        def weight_scale(dve, n, undo, stat, allmax):
            dve.tensor_reduce(rmax, chunk_max[:, 0:n], AX.X, ALU.max).then_inc(stat, 1)
            dve.wait_ge(allmax, 1)
            dve.tensor_scalar(gmax, gmax, 1e-30, None, ALU.max).then_inc(stat, 1)
            dve.wait_ge(stat, 2)
            dve.reciprocal(wsc, gmax).then_inc(stat, 1)
            dve.tensor_scalar(undo, gmax, 1.0 / (W_TOP * X_SCALE), None, ALU.mult).then_inc(stat, 1)
            dve.wait_ge(stat, 4)
            dve.tensor_scalar(wsc, wsc, W_TOP, None, ALU.mult).then_inc(stat, 1)
            dve.wait_ge(stat, 5)

        def prepare_attention(weights, w_out, is_b, masks, broadcasts):
            local, (w_raw,) = arena(("w_raw", [P, NK, 3 * D], F32))
            loaded = sem("qkv_loaded")
            other = sem("other_loaded")
            maxed = sem("qkv_max")
            stat = sem("qkv_scale_steps")
            allmax = sem("qkv_all_reduced")
            hi = sem("qkv_hi_done")
            lo = sem("qkv_lo_done")
            mask_step = sem("mask_step")
            fixed = sem("broadcasts_scaled")
            with nc.Block() as block:
                @block.sync
                def _(sp):
                    for w, o in weights:
                        sp.dma_start(w_raw[:, :, o:o + w.shape[1]], rows(w)).then_inc(loaded, 16)
                    sp.dma_start(wo[:], rows(w_out)).then_inc(other, 16)
                    for dst, src, _ in broadcasts:
                        sp.dma_start(dst, bcast(src)).then_inc(other, 16)
                    sp.wait_ge(other, 16 * (1 + len(broadcasts)))

                @block.gpsimd
                def _(pool):
                    if is_b:
                        pool.memset(masks[:], 0.0).then_inc(mask_step, 1)
                    else:
                        pool.iota(masks[:], pattern=[[1, S]], base=-(S - P), channel_multiplier=-1,
                                  allow_small_or_imprecise_dtypes=True).then_inc(mask_step, 1)
                    pool.wait_ge(mask_step, 1)
                    pool.affine_select(out=masks[:], in_=masks[:], compare_op=ALU.is_ge, fill=MASKED,
                                       base=S - P, pattern=[[-1, S]], channel_multiplier=1).then_inc(mask_step, 1)
                    pool.wait_ge(mask_step, 2)
                    pool.wait_ge(stat, 1)
                    pool.partition_all_reduce(gmax, rmax, P, RMAX).then_inc(allmax, 1)

                @block.scalar
                def _(act):
                    act.wait_ge(stat, 5)
                    for k in range(NK):
                        act.activation(qkv_hi[:, k, :], w_raw[:, k, :], ACT.Copy, scale=wsc).then_inc(hi, 1)

                @block.vector
                def _(dve):
                    dve.wait_ge(loaded, 16 * len(weights))
                    for k in range(NK):
                        dve.tensor_reduce(chunk_max[:, k:k + 1], w_raw[:, k, :], AX.X, ALU.max,
                                          apply_absolute_value=True).then_inc(maxed, 1)
                    dve.wait_ge(maxed, NK)
                    weight_scale(dve, NK, c_qkv, stat, allmax)
                    dve.tensor_scalar(c_q, c_qkv, HD ** -0.5, None, ALU.mult).then_inc(stat, 1)
                    for k in range(NK):
                        dve.wait_ge(hi, k + 1)
                        dve.scalar_tensor_tensor(out=qkv_lo[:, k, :], in0=w_raw[:, k, :], scalar=wsc,
                                                 in1=qkv_hi[:, k, :], op0=ALU.mult, op1=ALU.subtract)\
                            .then_inc(lo, 1)
                    dve.wait_ge(other, 16 * (1 + len(broadcasts)))
                    n = 0
                    for dst, _, factor in broadcasts:
                        if factor != 1.0:
                            dve.tensor_scalar(dst, dst, factor, None, ALU.mult).then_inc(fixed, 1)
                            n += 1
                    dve.wait_ge(fixed, n)
                    dve.wait_ge(lo, NK)
                    dve.wait_ge(stat, 6)
            local.close()
            end_phase()

        class Norm:

            def __init__(self, xn, x_hi, x_lo, stats):
                self.xn, self.x_hi, self.x_lo = xn, x_hi, x_lo
                self.raw = stats[:, 0:24].rearrange("p (i s) -> p i s", s=6)
                self.mv = stats[:, 24:32].rearrange("p (i s) -> p i s", s=2)
                self.var = stats[:, 32:36]
                self.rstd = stats[:, 36:40]
                self.stats = sem("bn_stats")
                self.aggr = sem("bn_aggr")
                self.eps = sem("eps_added")
                self.inv = sem("rstd_ready")
                self.xn_ready = sem("xn_ready")
                self.turned = sem("xn_turned")
                self.hi_done = sem("x_hi_done")
                self.lo_done = sem("x_lo_done")

            def normalise(self, dve, b):
                for i in range(NT):
                    dve.bn_stats(self.raw[:, i, :], x[:, bass.ds((b * NT + i) * D, D)]).then_inc(self.stats, 1)
                hold(dve, self.stats, b * NT + NT)
                for i in range(NT):
                    dve.bn_aggr(self.mv[:, i, :], self.raw[:, i, :]).then_inc(self.aggr, 1)
                dve.wait_ge(self.aggr, b * NT + NT)
                dve.tensor_scalar(self.var, self.mv[:, :, 1], EPS, None, ALU.add).then_inc(self.eps, 1)
                dve.wait_ge(self.inv, b + 1)
                for i in range(NT):
                    dve.tensor_scalar(self.xn[:, i, :], x[:, bass.ds((b * NT + i) * D, D)], self.mv[:, i, 0:1],
                                      self.rstd[:, i:i + 1], ALU.subtract, ALU.mult).then_inc(self.xn_ready, 1)

            def invert(self, pool, b):
                pool.wait_ge(self.eps, b + 1)
                pool.tensor_tensor(self.rstd, self.var, minus_half[:, 0:NT], ALU.pow).then_inc(self.inv, 1)

            def low(self, dve, b, k, src):
                dve.wait_ge(self.hi_done, b * NK + k + 1)
                dve.scalar_tensor_tensor(out=self.x_lo[:, k, :], in0=src[:], scalar=X_SCALE,
                                         in1=self.x_hi[:, k, :], op0=ALU.mult, op1=ALU.subtract)\
                    .then_inc(self.lo_done, 1)

            def high(self, act, b, k, src):
                act.wait_ge(self.turned, b * NK + k + 1)
                act.activation(self.x_hi[:, k, :], src[:], ACT.Copy, scale=X_SCALE).then_inc(self.hi_done, 1)

            def turn(self, pe, b, k, dst):
                pe.wait_ge(self.xn_ready, b * NT + NT)
                for i in range(NT):
                    t = pe.transpose(dst[:, i * P:(i + 1) * P], self.xn[:, i, k * P:(k + 1) * P], ident[:])
                t.then_inc(self.turned, 1)

        def attention(is_b, masks, lnw, slopes, bias_out):
            GROUPS = H // HPB
            PAIRS = HPB // 2
            UPB = HPB * UPH
            UPP = 2 * UPH
            TRI = NT * (NT + 1) // 2 * P
            local, (qkv, v_parts, split_q, split_k, q_t, k_t, s_buf, p_hi, p_lo, head_bias, x_parts,
                    stats) = arena(
                ("qk", [P, 2, NT, D], F32), ("v_parts", [P, NT, H, VW], BF16),
                ("split_q", [P, NT, P], F32R), ("split_k", [P, NT, P], F32R),
                ("q_t", [P, 2, S], F32R), ("k_t", [P, 2, S], F32R),
                ("s_buf", [P, TRI], F32), ("p_hi", [P, TRI], F16), ("p_lo", [P, TRI], F16),
                ("head_bias", [P, 2 if is_b else HPB, S], F32), ("x_parts", [P, 2, NK, S], F16),
                ("stats", [P, 144], F32))
            tmp = head_bias
            x_hi, x_lo = x_parts[:, 0], x_parts[:, 1]
            attn = x_parts[:].rearrange("p m k s -> p (m k s)").bitcast(F32).rearrange("p (i d) -> p i d", d=D)
            norm = Norm(qkv[:, 0], x_hi, x_lo, stats)
            neg_max = stats[:, 40:44]
            rsum = stats[:, 44:52]
            q_raw = stats[:, 52:100].rearrange("p (i s) -> p i s", s=6)
            q_mv = stats[:, 100:116].rearrange("p (i s) -> p i s", s=2)
            q_var = stats[:, 116:124]
            q_rstd = stats[:, 124:132]

            proj = sem("projected")
            evac = sem("qkv_bank_read")
            q_fixed = sem("qk_clipped")
            q_stats = sem("qk_bn_stats")
            q_aggr = sem("qk_bn_aggr")
            q_eps = sem("qk_eps")
            q_inv = sem("qk_rstd")
            q_norm = sem("qk_normed")
            q_gain = sem("qk_gained_pool")
            q_done = sem("qk_final_pool")
            q_gain_v = sem("qk_gained_vector")
            q_done_v = sem("qk_final_vector")
            v_ready = sem("v_ready")
            v_h = sem("v_high")
            v_r = sem("v_rest")
            v_m = sem("v_middle")
            v_l = sem("v_low")
            ones = sem("ones_set")
            sp_hi = sem("split_hi")
            sp_lo = sem("split_lo")
            bias_ready = sem("head_bias_ready")
            qk_turned = sem("qk_turned")
            qk_t_ready = sem("qk_t_ready")
            s_ready = sem("scores_ready")
            s_masked = sem("scores_masked")
            p_ready = sem("probs_ready")
            p_turned = sem("probs_turned")
            hi_ready = sem("probs_hi")
            lo_ready = sem("probs_lo")
            pv_done = sem("pair_values_done")
            pv_sum = sem("pair_summed")
            r_ready = sem("rsum_ready")
            o_ready = sem("pair_out")
            o_turned = sem("o_turned")
            o_t_ready = sem("o_t_ready")
            out_ready = sem("out_ready")
            x_added = sem("x_added")
            bo_added = sem("bo_added")

            FREE = {s_masked: UPB, lo_ready: 3, p_turned: 3, pv_sum: 4, qk_t_ready: 2, qk_turned: 2, x_added: NT}

            def wait(engine, semaphore, count):
                engine.wait_ge(semaphore, count + FREE.get(semaphore, 0))

            def tile(n):
                return NT - 1 - n % UPH

            def span(n):
                i = tile(n)
                return slice(i * (i + 1) // 2 * P, (i + 1) * (i + 2) // 2 * P)

            P_BANKS = (bank[2], bank[3], bank[4])
            PV_BANKS = (bank[5], bank[6])
            TURN_BANK = bank[7]
            BLOCKS = ((0,), (1,), (2, 3))

            def is_block(n):
                return n % UPH in (0, 1, 3)

            def block_of(b, hg, n):
                return ((b * GROUPS + hg) * HPB + n // UPH) * 3 + (0, 1, None, 2)[n % UPH]

            def block_bank(n):
                return P_BANKS[(0, 1, None, 2)[n % UPH]]

            def block_units(n):
                return [n // UPH * UPH + u for u in BLOCKS[(0, 1, None, 2)[n % UPH]]]

            def block_span(n):
                return slice(min(span(u).start for u in block_units(n)), max(span(u).stop for u in block_units(n)))

            def turned_probs(n):
                return block_bank(n)[:, 0:block_span(n).stop - block_span(n).start]

            T_LAG, HI_LAG, LO_LAG, V_LAG = 1, 3, 4, 5
            TURN_STEPS = (1, 3)
            OUT_STEP = 6

            with nc.Block() as block:
                @block.tensor
                def _(pe):
                    def project(b):
                        for u in range(3 * NT):
                            i, g = u // 3, u % 3
                            if u == 0:
                                pe.wait_ge(norm.lo_done, b * NK + NK)
                            if u == 2:
                                wait(pe, x_added, b * NT)
                            if u >= 8:
                                pe.wait_ge(evac, b * 12 + u - 7)
                            n = 0
                            for k in range(NK):
                                for xs, ws in ((x_hi, qkv_hi), (x_lo, qkv_hi), (x_hi, qkv_lo)):
                                    t = pe.matmul(bank[u % 8][:], xs[:, k, i * P:(i + 1) * P],
                                                  ws[:, k, g * D:(g + 1) * D], start=(n == 0),
                                                  stop=(n == 3 * NK - 1))
                                    n += 1
                            t.then_inc(proj, 1)
                        pe.wait_ge(evac, b * 12 + 12)
                        hold(pe, v_l, b * NT + NT)

                    def turn_pair(b, hg, pp, g):
                        pair = (b * GROUPS + hg) * PAIRS + pp
                        pe.wait_ge(sp_lo, 2 * pair + g + 1)
                        wait(pe, qk_t_ready, 2 * pair + g)
                        for i in range(NT):
                            t = pe.transpose(TURN_BANK[:, i * P:(i + 1) * P],
                                             (split_q, split_k)[g][:, i, :].bitcast(F32), ident[:])
                        t.then_inc(qk_turned, 1)

                    def scores(b, hg, n):
                        unit = (b * GROUPS + hg) * UPB + n
                        i = tile(n)
                        if n % UPP == 0:
                            pair = (b * GROUPS + hg) * PAIRS + n // UPP
                            wait(pe, qk_t_ready, 2 * pair + 2)
                        wait(pe, s_masked, unit - 1)
                        slot = n // UPP % 2
                        r = 64 * (n // UPH % 2)
                        pe.matmul(bank[n % 2][:, 0:(i + 1) * P], q_t[r:r + 64, slot, i * P:(i + 1) * P],
                                  k_t[r:r + 64, slot, 0:(i + 1) * P], start=True, stop=True).then_inc(s_ready, 1)

                    def turn_probs(b, hg, n):
                        pe.wait_ge(p_ready, (b * GROUPS + hg) * UPB + n + 1)
                        wait(pe, lo_ready, block_of(b, hg, n) - 2)
                        src, dst = s_buf[:, block_span(n)], turned_probs(n)
                        for j in range(dst.shape[1] // P):
                            t = pe.transpose(dst[:, j * P:(j + 1) * P], src[:, j * P:(j + 1) * P], ident[:])
                        t.then_inc(p_turned, 1)

                    def values(b, hg, n):
                        if n % UPP == 0:
                            wait(pe, pv_sum, 2 * ((b * GROUPS + hg) * PAIRS + n // UPP) - 2)
                        wait(pe, lo_ready, block_of(b, hg, n) + 1)
                        for u in block_units(n):
                            i = tile(u)
                            o = (n // UPH % 2 * NT + i) * VW
                            m = 0
                            for j in range(i + 1):
                                for part in (p_hi, p_lo):
                                    t = pe.matmul(PV_BANKS[n // UPP % 2][:, o:o + VW],
                                                  part[:, span(u)][:, j * P:(j + 1) * P],
                                                  v_parts[:, j, bass.ds(hg * HPB + n // UPH, 1), :],
                                                  start=(m == 0), stop=(m == 2 * i + 1))
                                    m += 1
                        if n % UPP == UPP - 1:
                            t.then_inc(pv_done, 1)

                    def group(b, hg, first=False, last=False):
                        if first:
                            turn_pair(b, hg, 0, 0)
                            turn_pair(b, hg, 0, 1)
                            scores(b, hg, 0)
                            scores(b, hg, 1)
                        for n in range(UPB):
                            if n % UPP in TURN_STEPS and not (last and n + UPP >= UPB):
                                turn_pair(b, hg, n // UPP + 1, TURN_STEPS.index(n % UPP))
                            if n + 2 < UPB or not last:
                                scores(b, hg, n + 2)
                            if is_block(n - V_LAG) and (n >= V_LAG or not first):
                                values(b, hg, n - V_LAG)
                            if is_block(n - T_LAG) and (n >= T_LAG or not first):
                                turn_probs(b, hg, n - T_LAG)
                        if last:
                            for n in range(UPB, UPB + V_LAG):
                                if is_block(n - V_LAG):
                                    values(b, hg, n - V_LAG)
                                if n < UPB + T_LAG and is_block(n - T_LAG):
                                    turn_probs(b, hg, n - T_LAG)

                    def output(b):
                        def turn_out(i):
                            for k in range(NK):
                                t = pe.transpose(bank[i % 2][:, k * P:(k + 1) * P],
                                                 attn[:, i, k * P:(k + 1) * P], ident[:])
                            t.then_inc(o_turned, 1)

                        pe.wait_ge(o_ready, (b + 1) * (H // 2))
                        turn_out(0)
                        for i in range(NT):
                            if i + 1 < NT:
                                turn_out(i + 1)
                            pe.wait_ge(o_t_ready, b * NT + i + 1)
                            if i >= 2:
                                wait(pe, x_added, b * NT + i - 1)
                            for k in range(NK):
                                t = pe.matmul(bank[2 + i % 2][:], s_buf[:, i % 2 * D + k * P:i % 2 * D + (k + 1) * P],
                                              wo[:, k, :], start=(k == 0), stop=(k == NK - 1))
                            t.then_inc(out_ready, 1)

                    with pe.Fori(0, B) as b:
                        for k in range(NK):
                            norm.turn(pe, b, k, bank[4 + k])
                        project(b)
                        group(b, 0, first=True)
                        with pe.Fori(1, GROUPS - 1) as hg:
                            group(b, hg)
                        group(b, GROUPS - 1, last=True)
                        output(b)

                @block.scalar
                def _(act):
                    def project(b):
                        for i in range(NT):
                            if not is_b:
                                for g in range(3):
                                    act.wait_ge(proj, b * 12 + 3 * i + g + 1)
                                    if g == 2 and i >= 1:
                                        act.wait_ge(v_l, b * NT + i)
                                    dst = qkv[:, g, i, :] if g < 2 else tmp[:, 0, :]
                                    act.activation(dst, bank[(3 * i + g) % 8][:], ACT.Copy, scale=c_qkv)\
                                        .then_inc(evac, 1)
                            vv = v_parts[:, i, :, :]
                            act.wait_ge(v_ready, b * NT + i + 1)
                            act.copy(vv[:, :, 0:HD], tmp[:, 0, :].rearrange("p (h d) -> p h d", d=HD))\
                                .then_inc(v_h, 1)
                            act.wait_ge(v_r, b * NT + i + 1)
                            act.copy(vv[:, :, HD:2 * HD], tmp[:, 1, :].rearrange("p (h d) -> p h d", d=HD))\
                                .then_inc(v_m, 1)

                    def copy_pair(b, hg, pp, g):
                        pair = (b * GROUPS + hg) * PAIRS + pp
                        wait(act, qk_turned, 2 * pair + g + 1)
                        act.copy((q_t, k_t)[g][:, pp % 2, :], TURN_BANK[:]).then_inc(qk_t_ready, 1)

                    def exps(b, hg, n):
                        unit = (b * GROUPS + hg) * UPB + n
                        wait(act, s_masked, unit + 1)
                        act.activation(s_buf[:, span(n)], s_buf[:, span(n)], ACT.Exp,
                                       bias=neg_max[:, n % 4:n % 4 + 1], scale=-1.0).then_inc(p_ready, 1)

                    def highs(b, hg, n):
                        wait(act, p_turned, block_of(b, hg, n) + 1)
                        act.copy(p_hi[:, block_span(n)], turned_probs(n)).then_inc(hi_ready, 1)

                    def group(b, hg, first=False, last=False):
                        if first:
                            copy_pair(b, hg, 0, 0)
                            copy_pair(b, hg, 0, 1)
                        for n in range(UPB):
                            exps(b, hg, n)
                            if is_block(n - HI_LAG) and (n >= HI_LAG or not first):
                                highs(b, hg, n - HI_LAG)
                            if n % UPP in TURN_STEPS and not (last and n + UPP >= UPB):
                                copy_pair(b, hg, n // UPP + 1, TURN_STEPS.index(n % UPP))
                        if last:
                            for n in range(UPB - HI_LAG, UPB):
                                if is_block(n):
                                    highs(b, hg, n)

                    with act.Fori(0, B) as b:
                        for k in range(NK):
                            norm.high(act, b, k, bank[4 + k])
                        project(b)
                        group(b, 0, first=True)
                        with act.Fori(1, GROUPS - 1) as hg:
                            group(b, hg)
                        group(b, GROUPS - 1, last=True)
                        for i in range(NT):
                            act.wait_ge(o_turned, b * NT + i + 1)
                            act.copy(s_buf[:, i % 2 * D:(i % 2 + 1) * D], bank[i % 2][:]).then_inc(o_t_ready, 1)

                @block.vector
                def _(dve):
                    for semaphore, count in FREE.items():
                        dve.sem_inc(semaphore, count)

                    def qk_normalise(b, i):
                        dve.wait_ge(q_inv, b * NT + i + 1)
                        for g in range(2):
                            n = 2 * i + g
                            dve.tensor_scalar(qkv[:, g, i, :], qkv[:, g, i, :], q_mv[:, n, 0:1],
                                              q_rstd[:, n:n + 1], ALU.subtract, ALU.mult).then_inc(q_norm, 1)

                    def project(b):
                        for i in range(NT):
                            for g in range(3):
                                u = 3 * i + g
                                dst = qkv[:, g, i, :] if g < 2 else tmp[:, 0, :]
                                if is_b:
                                    dve.wait_ge(proj, b * 12 + u + 1)
                                    if g == 2 and i >= 1:
                                        dve.wait_ge(v_l, b * NT + i)
                                    t = dve.scalar_tensor_tensor(
                                        out=dst, in0=bank[u % 8][:], scalar=c_q if g == 0 else c_qkv,
                                        in1=lnw[:, g, :], op0=ALU.mult, op1=ALU.add)
                                    t.then_inc(evac, 1)
                                    if g == 2:
                                        dve.wait_ge(evac, b * 12 + u + 1)
                                        dve.sem_inc(v_ready, 1)
                                else:
                                    dve.wait_ge(evac, b * 12 + u + 1)
                                    dve.tensor_scalar(dst, dst, CLIP, -CLIP, ALU.min, ALU.max)\
                                        .then_inc(v_ready if g == 2 else q_fixed, 1)
                                    if g < 2:
                                        dve.wait_ge(q_fixed, b * 8 + 2 * i + g + 1)
                                        dve.bn_stats(q_raw[:, 2 * i + g, :], dst).then_inc(q_stats, 1)
                                    if g == 1:
                                        hold(dve, q_stats, b * 8 + 2 * i + 2)
                                        for n in (2 * i, 2 * i + 1):
                                            dve.bn_aggr(q_mv[:, n, :], q_raw[:, n, :]).then_inc(q_aggr, 1)
                                        dve.wait_ge(q_aggr, b * 8 + 2 * i + 2)
                                        dve.tensor_scalar(q_var[:, 2 * i:2 * i + 2], q_mv[:, 2 * i:2 * i + 2, 1],
                                                          EPS, None, ALU.add).then_inc(q_eps, 1)
                            vv = v_parts[:, i, :, :]
                            t0 = tmp[:, 0, :].rearrange("p (h d) -> p h d", d=HD)
                            t1 = tmp[:, 1, :].rearrange("p (h d) -> p h d", d=HD)
                            dve.wait_ge(v_h, b * NT + i + 1)
                            dve.tensor_tensor(t1, t0, vv[:, :, 0:HD], ALU.subtract).then_inc(v_r, 1)
                            if not is_b:
                                qk_normalise(b, i)
                            dve.wait_ge(v_m, b * NT + i + 1)
                            dve.tensor_tensor(vv[:, :, 2 * HD:3 * HD], t1, vv[:, :, HD:2 * HD], ALU.subtract)\
                                .then_inc(v_l, 1)
                        if not is_b:
                            i = NT - 1
                            dve.wait_ge(q_norm, b * 8 + 8)
                            for g in range(2):
                                dve.tensor_tensor(qkv[:, g, i, :], qkv[:, g, i, :], lnw[:, g, :], ALU.mult)\
                                    .then_inc(q_gain_v, 1)
                            for g in range(2):
                                dve.wait_ge(q_gain_v, b * 2 + g + 1)
                                dve.tensor_tensor(qkv[:, g, i, :], qkv[:, g, i, :], lnw[:, 2 + g, :], ALU.add)\
                                    .then_inc(q_done_v, 1)

                    def mask_max(b, hg, n):
                        unit = (b * GROUPS + hg) * UPB + n
                        w = (tile(n) + 1) * P
                        if not is_b and n % UPH == 0:
                            dve.wait_ge(bias_ready, (b * GROUPS + hg) * HPB + n // UPH + 1)
                        if n % UPH == 2:
                            wait(dve, p_turned, ((b * GROUPS + hg) * HPB + n // UPH) * 3)
                        hold(dve, s_ready, unit + 1)
                        table = masks[:, S - w:S] if is_b else head_bias[:, n // UPH, S - w:S]
                        dve.tensor_tensor_reduce(out=s_buf[:, span(n)], in0=bank[n % 2][:, 0:w], in1=table,
                                                 scale=-1.0, scalar=BIG, op0=ALU.add, op1=ALU.min,
                                                 accum_out=neg_max[:, n % 4:n % 4 + 1]).then_inc(s_masked, 1)

                    def lows(b, hg, n):
                        dve.wait_ge(hi_ready, block_of(b, hg, n) + 1)
                        dve.tensor_tensor(p_lo[:, block_span(n)], turned_probs(n), p_hi[:, block_span(n)], ALU.subtract)\
                            .then_inc(lo_ready, 1)

                    def pair_sum(b, hg, pp):
                        dve.wait_ge(pv_done, (b * GROUPS + hg) * PAIRS + pp + 1)
                        src = PV_BANKS[pp % 2][:, 0:2 * NT * VW].rearrange("p (i v) -> p i v", v=VW)
                        dve.reciprocal(rsum, src[:, :, 3 * HD]).then_inc(r_ready, 1)
                        parts = src[:, :, 0:3 * HD].rearrange("p (h i) (t c) -> p h i c t", h=2, t=3)
                        for h in range(2):
                            dve.tensor_reduce(attn[:, :, bass.ds((hg * HPB + 2 * pp + h) * HD, HD)],
                                              parts[:, h], AX.X, ALU.add).then_inc(pv_sum, 1)

                    def pair_out(b, hg, pp):
                        pair = (b * GROUPS + hg) * PAIRS + pp
                        dve.wait_ge(r_ready, pair + 1)
                        wait(dve, pv_sum, 2 * pair + 2)
                        cols = attn[:, :, bass.ds((hg * HPB + 2 * pp) * HD, 2 * HD)]\
                            .rearrange("p i (h c) -> p i h c", h=2)
                        rs = rsum.rearrange("p (h i) -> p i h", h=2).unsqueeze(3).to_broadcast([P, NT, 2, HD])
                        dve.tensor_tensor(cols, cols, rs, ALU.mult).then_inc(o_ready, 1)

                    def group(b, hg, first=False, last=False):
                        for n in range(UPB):
                            mask_max(b, hg, n)
                            if is_block(n - LO_LAG) and (n >= LO_LAG or not first):
                                lows(b, hg, n - LO_LAG)
                            if n >= UPP or not first:
                                if n % UPP == OUT_STEP:
                                    pair_sum(b, hg, n // UPP - 1)
                                if n % UPP == OUT_STEP + 1:
                                    pair_out(b, hg, n // UPP - 1)
                        if last:
                            for n in range(UPB - LO_LAG, UPB):
                                if is_block(n):
                                    lows(b, hg, n)
                            pair_sum(b, hg, PAIRS - 1)
                            pair_out(b, hg, PAIRS - 1)

                    with dve.Fori(0, B) as b:
                        norm.normalise(dve, b)
                        for k in range(NK):
                            norm.low(dve, b, k, bank[4 + k])
                        project(b)
                        group(b, 0, first=True)
                        with dve.Fori(1, GROUPS - 1) as hg:
                            group(b, hg)
                        group(b, GROUPS - 1, last=True)
                        for i in range(NT):
                            dve.wait_ge(out_ready, b * NT + i + 1)
                            if is_b and i == 0:
                                dve.wait_ge(bo_added, b * NT + NT)
                            xt = x[:, bass.ds((b * NT + i) * D, D)]
                            dve.tensor_tensor(xt, bank[2 + i % 2][:], xt, ALU.add).then_inc(x_added, 1)

                @block.gpsimd
                def _(pool):
                    for i in range(NT):
                        t = pool.memset(v_parts[:, i, :, 3 * HD:VW], 1.0)
                    t.then_inc(ones, 1)
                    pool.wait_ge(ones, 1)

                    def gain(b, i):
                        pool.wait_ge(q_norm, b * 8 + 2 * i + 2)
                        for g in range(2):
                            pool.tensor_tensor(qkv[:, g, i, :], qkv[:, g, i, :], lnw[:, g, :], ALU.mult)\
                                .then_inc(q_gain, 1)
                        for g in range(2):
                            pool.wait_ge(q_gain, (b * (NT - 1) + i) * 2 + g + 1)
                            pool.tensor_tensor(qkv[:, g, i, :], qkv[:, g, i, :], lnw[:, 2 + g, :], ALU.add)\
                                .then_inc(q_done, 1)

                    def split(b, hg, pp, g):
                        pair = (b * GROUPS + hg) * PAIRS + pp
                        wait(pool, qk_turned, 2 * pair + g - 1)
                        src = qkv[:, g, :, bass.ds((hg * HPB + 2 * pp) * HD, 2 * HD)]\
                            .rearrange("p i (h d) -> p i h d", h=2)
                        to = (split_q, split_k)[g][:].rearrange("p i (h m d) -> p i h m d", h=2, m=4)
                        highs, lows = ((0, 2), (1, 3)) if g == 0 else ((0, 1), (2, 3))
                        for m in highs:
                            t = pool.tensor_copy(to[:, :, :, m, :], src)
                        t.then_inc(sp_hi, 1)
                        hold(pool, sp_hi, 2 * pair + g + 1)
                        for m in lows:
                            t = pool.tensor_tensor(to[:, :, :, m, :], src, to[:, :, :, highs[1], :], ALU.subtract)
                        t.then_inc(sp_lo, 1)

                    def biases_of(b, hg, h):
                        head = (b * GROUPS + hg) * HPB + h
                        hold(pool, s_masked, UPH * (head - HPB + 1) + FREE[s_masked])
                        pool.tensor_tensor(head_bias[:, h, :], masks[:],
                                           slopes[:, bass.ds(hg * HPB + h, 1)].to_broadcast([P, S]), ALU.mult)\
                            .then_inc(bias_ready, 1)

                    with pool.Fori(0, B) as b:
                        norm.invert(pool, b)
                        if is_b:
                            hold(pool, norm.xn_ready, b * NT + NT)
                            for i in range(NT):
                                xt = x[:, bass.ds((b * NT + i) * D, D)]
                                pool.tensor_tensor(xt, xt, bias_out[:], ALU.add).then_inc(bo_added, 1)
                            hold(pool, evac, b * 12 + 12)
                        else:
                            for i in range(NT):
                                hold(pool, q_eps, b * NT + i + 1)
                                pool.tensor_tensor(q_rstd[:, 2 * i:2 * i + 2], q_var[:, 2 * i:2 * i + 2],
                                                   minus_half[:, 0:2], ALU.pow).then_inc(q_inv, 1)
                                if i >= 1:
                                    gain(b, i - 1)
                            pool.wait_ge(q_done, (b + 1) * 2 * (NT - 1))
                            hold(pool, q_done_v, b * 2 + 2)
                        with pool.Fori(0, GROUPS) as hg:
                            for pp in range(PAIRS):
                                for g in range(2):
                                    split(b, hg, pp, g)
                                    if not is_b:
                                        biases_of(b, hg, 2 * pp + g)
            local.close()
            end_phase()

        def ffn(last_layer):
            local, (xn, x_hi, x_lo, dn_hi, dn_lo, sig, hid, h_hi, h_lo, stats) = arena(
                ("xn", [P, NT, D], F32), ("fx_hi", [P, NK, S], F16), ("fx_lo", [P, NK, S], F16),
                ("dn_hi", [P, NC, D], F32R), ("dn_lo", [P, NC, D], F32R),
                ("sig", [P, 2, S], F32), ("hid", [P, 2, S], F32),
                ("h_hi", [P, 2, S], F32R), ("h_lo", [P, 2, S], F32R), ("fstats", [P, 48], F32))
            norm = Norm(xn[:], x_hi, x_lo, stats)
            dhi = sem("down_hi")
            dlo = sem("down_lo")
            gate_ready = sem("gate_ready")
            up_ready = sem("up_ready")
            sig_ready = sem("silu_ready")
            hid_ready = sem("hidden_ready")
            hhi = sem("hidden_hi")
            hlo = sem("hidden_lo")
            down = sem("down_used")
            x_added = sem("ffn_x_added")
            stored = sem("stored")
            out_v = out.rearrange("(t p) d -> p t d", p=P)
            x_v = x[:].rearrange("p (t d) -> p t d", d=D)
            turn_banks = [bank[6], bank[7], bank[4], bank[5]]
            PAIRS = (NC - 3) // 2

            with nc.Block() as block:
                @block.tensor
                def _(pe):
                    def gate_up(b, c, s):
                        for g in range(2):
                            n = 0
                            for k in range(NK):
                                for ws, xs in ((gu_hi, x_hi), (gu_hi, x_lo), (gu_lo, x_hi)):
                                    t = pe.matmul(bank[4 + 2 * s + g][:], ws[:, k, g, bass.ds(c * P, P)], xs[:, k, :],
                                                  start=(n == 0), stop=(n == 3 * NK - 1))
                                    n += 1
                            t.then_inc(up_ready if g else gate_ready, 1)

                    def contract(b, c, s, first=False, end=False):
                        pe.wait_ge(hlo, b * NC + c + 1)
                        for i in range(NT):
                            for m, (hs, ws) in enumerate(((h_hi, dn_hi), (h_lo, dn_hi), (h_hi, dn_lo))):
                                t = pe.matmul(bank[i][:], hs[:, s, i * P:(i + 1) * P], ws[:, bass.ds(c, 1), :],
                                              start=(first and m == 0), stop=(end and m == 2))
                        t.then_inc(down, 1)

                    def batch(b, begin, more):
                        if begin:
                            for k in range(NK):
                                norm.turn(pe, b, k, turn_banks[k])
                        pe.wait_ge(norm.lo_done, b * NK + NK)
                        gate_up(b, 0, 0)
                        gate_up(b, 1, 1)
                        if not begin:
                            pe.wait_ge(x_added, b * NT)
                        contract(b, 0, 0, first=True)
                        with pe.Fori(0, PAIRS) as j:
                            for s in range(2):
                                c = 2 * j + 2 + s
                                pe.wait_ge(hid_ready, b * NC + c - 1)
                                gate_up(b, c, s)
                                contract(b, c - 1, 1 - s)
                        pe.wait_ge(hid_ready, b * NC + NC - 2)
                        gate_up(b, NC - 1, 0)
                        contract(b, NC - 2, 1)
                        if more:
                            for k in (0, 1):
                                norm.turn(pe, b + 1, k, turn_banks[k])
                            pe.wait_ge(hid_ready, b * NC + NC)
                            for k in (2, 3):
                                norm.turn(pe, b + 1, k, turn_banks[k])
                        contract(b, NC - 1, 0, end=True)

                    pe.wait_ge(dlo, NC)
                    batch(0, True, True)
                    with pe.Fori(1, B - 1) as b:
                        batch(b, False, True)
                    batch(B - 1, False, False)

                @block.scalar
                def _(act):
                    def chunk(b, c, s, free=True):
                        act.wait_ge(gate_ready, b * NC + c + 1)
                        act.activation(sig[:, s, :], bank[4 + 2 * s][:], ACT.Silu, scale=c_gu[:]).then_inc(sig_ready, 1)
                        act.wait_ge(hid_ready, b * NC + c + 1)
                        if free:
                            act.wait_ge(down, b * NC + c - 1)
                        act.copy(h_hi[:, s, :], hid[:, s, :]).then_inc(hhi, 1)

                    def batch(b, begin, more):
                        if begin:
                            for k in range(NK):
                                norm.high(act, b, k, turn_banks[k])
                        chunk(b, 0, 0, free=not begin)
                        chunk(b, 1, 1, free=not begin)
                        with act.Fori(0, PAIRS) as j:
                            for s in range(2):
                                chunk(b, 2 * j + 2 + s, s)
                        chunk(b, NC - 1, 0)
                        if more:
                            for k in range(NK):
                                norm.high(act, b + 1, k, turn_banks[k])

                    for c in range(NC):
                        act.copy(dn_hi[:, c, :], w_down[:, c, :]).then_inc(dhi, 1)
                    batch(0, True, True)
                    with act.Fori(1, B - 1) as b:
                        batch(b, False, True)
                    batch(B - 1, False, False)

                @block.vector
                def _(dve):
                    def chunk(b, c, s):
                        dve.wait_ge(sig_ready, b * NC + c + 1)
                        dve.wait_ge(up_ready, b * NC + c + 1)
                        dve.scalar_tensor_tensor(out=hid[:, s, :], in0=bank[5 + 2 * s][:], scalar=c_gu[:],
                                                 in1=sig[:, s, :], op0=ALU.mult, op1=ALU.mult)\
                            .then_inc(hid_ready, 1)
                        dve.wait_ge(hhi, b * NC + c + 1)
                        dve.tensor_tensor(h_lo[:, s, :], hid[:, s, :], h_hi[:, s, :].bitcast(F32), ALU.subtract)\
                            .then_inc(hlo, 1)

                    def batch(b, begin, more):
                        if begin:
                            norm.normalise(dve, b)
                            for k in range(NK):
                                norm.low(dve, b, k, turn_banks[k])
                        chunk(b, 0, 0)
                        chunk(b, 1, 1)
                        if more:
                            norm.normalise(dve, b + 1)
                        with dve.Fori(0, PAIRS) as j:
                            for s in range(2):
                                chunk(b, 2 * j + 2 + s, s)
                        chunk(b, NC - 1, 0)
                        if more:
                            for k in range(NK):
                                norm.low(dve, b + 1, k, turn_banks[k])
                        dve.wait_ge(down, b * NC + NC)
                        for i in range(NT):
                            xt = x[:, bass.ds((b * NT + i) * D, D)]
                            dve.tensor_tensor(xt, bank[i][:], xt, ALU.add).then_inc(x_added, 1)

                    for c in range(NC):
                        dve.wait_ge(dhi, c + 1)
                        dve.tensor_tensor(dn_lo[:, c, :], w_down[:, c, :], dn_hi[:, c, :].bitcast(F32), ALU.subtract)\
                            .then_inc(dlo, 1)
                    batch(0, True, True)
                    with dve.Fori(1, B - 1) as b:
                        batch(b, False, True)
                    batch(B - 1, False, False)

                @block.gpsimd
                def _(pool):
                    with pool.Fori(0, B) as b:
                        norm.invert(pool, b)

                if last_layer:
                    @block.sync
                    def _(sp):
                        with sp.Fori(0, B) as b:
                            sp.wait_ge(x_added, b * NT + NT)
                            sp.dma_start(out_v[:, bass.ds(b * NT, NT), :], x_v[:, bass.ds(b * NT, NT), :])\
                                .then_inc(stored, 16)
                        sp.wait_ge(stored, 16 * B)
            local.close()
            end_phase()

        prepare()
        qkv_hi = sb("qkv_hi", [P, NK, 3 * D], F16)
        qkv_lo = sb("qkv_lo", [P, NK, 3 * D], F16)
        wo = sb("wo", [P, NK, D], F32)
        phase = ExitStack()
        masks = phase.enter_context(nc.sbuf_tensor("masks", [P, S], F32))
        lnw = phase.enter_context(nc.sbuf_tensor("lnw", [P, 4, D], F32))
        slopes = phase.enter_context(nc.sbuf_tensor("slopes", [P, H], F32))
        prepare_attention([(a["Wqkv_t"], 0)], a["Wout_t"], False, masks,
                          [(lnw[:, 0, :], a["q_ln_w"], HD ** -0.5), (lnw[:, 1, :], a["k_ln_w"], 1.0),
                           (lnw[:, 2, :], a["q_ln_b"], HD ** -0.5), (lnw[:, 3, :], a["k_ln_b"], 1.0),
                           (slopes[:], a["alibi_slopes"], 1.0)])
        attention(False, masks, lnw, slopes, None)
        phase.close()
        ffn(False)
        phase = ExitStack()
        masks = phase.enter_context(nc.sbuf_tensor("masks_b", [P, S], F32))
        biases = phase.enter_context(nc.sbuf_tensor("biases", [P, 3, D], F32))
        bias_out = phase.enter_context(nc.sbuf_tensor("bias_out", [P, D], F32))
        prepare_attention([(a["Wq_t"], 0), (a["Wk_t"], D), (a["Wv_t"], 2 * D)], a["Wo_t"], True, masks,
                          [(biases[:, 0, :], a["bq"], HD ** -0.5), (biases[:, 1, :], a["bk"], 1.0),
                           (biases[:, 2, :], a["bv"], 1.0), (bias_out[:], a["bo"], 1.0)])
        attention(True, masks, biases, None, bias_out)
        phase.close()
        ffn(True)


def kernel(**inputs):
    import numpy as np
    import concourse.bacc as bacc
    from concourse.bass_utils import run_bass_kernel_spmd

    def get(name):
        return np.asarray(inputs[name])

    def turned(name):
        return np.ascontiguousarray(get(name).T)

    x = get("L0_attn_a_hidden_states")
    arrays = {
        "x": np.ascontiguousarray(x.reshape(-1, x.shape[-1])),
        "Wqkv_t": turned("L0_attn_a_Wqkv"),
        "Wout_t": turned("L0_attn_a_Wout"),
        "Wq_t": turned("L0_attn_b_Wq"),
        "Wk_t": turned("L0_attn_b_Wk"),
        "Wv_t": turned("L0_attn_b_Wv"),
        "Wo_t": turned("L0_attn_b_Wo"),
        "gate_q_t": turned("L0_ffn_gate_q"),
        "up_q_t": turned("L0_ffn_up_q"),
        "down_q_t": turned("L0_ffn_down_q"),
        "gate_A_t": turned("L0_ffn_gate_A"),
        "up_A_t": turned("L0_ffn_up_A"),
        "down_A_t": turned("L0_ffn_down_A"),
    }
    for name in ("q_ln_w", "q_ln_b", "k_ln_w", "k_ln_b"):
        arrays[name] = get(f"L0_attn_a_{name}")
    for name in ("bq", "bk", "bv", "bo"):
        arrays[name] = get(f"L0_attn_b_{name}")
    for name in ("gate_scale", "gate_B", "up_scale", "up_B", "down_scale", "down_B"):
        arrays[name] = get(f"L0_ffn_{name}")
    arrays["alibi_slopes"] = (1.0 / np.power(2.0, np.arange(1, H + 1, dtype=np.float32) * np.float32(8.0 / H)))\
        .astype(np.float32)

    nc = bacc.Bacc("TRN2", target_bir_lowering=False, num_devices=1)
    args = {name: nc.dram_tensor(f"in_{name}", v.shape, mybir.dt.from_np(v.dtype), kind="ExternalInput").ap()
            for name, v in arrays.items()}
    out = nc.dram_tensor("out_0", (B * S, D), F32, kind="ExternalOutput").ap()
    program(nc, args, out)
    r = run_bass_kernel_spmd(nc, [{f"in_{n}": v for n, v in arrays.items()}], core_ids=[0])
    return r.results[0]["out_0"].reshape(x.shape)
```

```python
from contextlib import ExitStack

import concourse.bass as bass
from concourse import mybir

F32 = mybir.dt.float32
F32R = mybir.dt.float32r
F16 = mybir.dt.float16
BF16 = mybir.dt.bfloat16
I32 = mybir.dt.int32
ALU = mybir.AluOpType
ACT = mybir.ActivationFunctionType
AX = mybir.AxisListType
RMAX = bass.bass_isa.ReduceOp.max

P = 128
B, S, D = 4, 512, 512
H, HD = 32, 16
I_FFN, RANK = 1376, 32
NT = S // P
NK = D // P
NC = -(-I_FFN // P)
IP = NC * P
CLIP = 8.0
EPS = 1e-5
LR_SCALE, Q_ZERO, Q_STEP = 0.02, 7.5, 0.005
X_SCALE = 2048.0
W_TOP = 30000.0
MASKED = -1e32
HPB = 4
UPH = NT
VW = 3 * HD + 1
BIG = 3e38


def program(nc, a, out):
    ctx = ExitStack()
    with ctx:
        def sb(name, shape, dt):
            return ctx.enter_context(nc.sbuf_tensor(name, shape, dt))

        sem_count = [0]

        phase_sems = []

        def sem_all(name):
            return ctx.enter_context(nc.semaphore(name))

        def sem(name):
            sem_count[0] += 1
            phase_sems.append(nc.alloc_semaphore(name=f"{name}_{sem_count[0]}"))
            return phase_sems[-1]

        def end_phase():
            numbers = sorted(s.num for s in phase_sems)
            runs = [[n, n + 1] for n in numbers if n - 1 not in numbers]
            for run in runs:
                while run[1] in numbers:
                    run[1] += 1
            with nc.Block() as block:
                @block.sync
                def _(sp):
                    for first, end in runs:
                        sp.sem_clear(range(first, end))
            for s in phase_sems:
                nc.release_semaphore(s)
            phase_sems.clear()

        bank = [ctx.enter_context(nc.psum_tensor(f"bank{i}", [P, 512], F32)) for i in range(8)]

        x = sb("x", [P, B * NT * D], F32)
        ident = sb("ident", [P, P], F32)
        gu_hi = sb("gu_hi", [P, NK, 2, IP], F16)
        gu_lo = sb("gu_lo", [P, NK, 2, IP], F16)
        down_dram = nc.dram_tensor("down_weights", (P, NC, D), F32).ap()
        minus_half = sb("minus_half", [P, 2 * NT], F32)
        c_gu = sb("c_gu", [P, 1], F32)
        small = sb("small", [P, 64], F32)
        gmax, rmax, wsc, c_qkv, c_q, w_gu_scale = (small[:, i:i + 1] for i in range(6))
        chunk_max = small[:, 8:32]

        def arena(*specs):
            local = ExitStack()
            sem_count[0] += 1
            return local, [local.enter_context(nc.sbuf_tensor(f"{n}_{sem_count[0]}", s, d)) for n, s, d in specs]

        waits_over = sem_all("waits_over")

        def hold(engine, semaphore, value):
            engine.wait_ge(semaphore, value)
            engine.sem_inc(waits_over, 1)

        def rows(w):
            return w.rearrange("(k p) n -> p k n", p=P)

        def bcast(v):
            return v.rearrange("(a n) -> a n", a=1).partition_broadcast(P)

        def prepare():
            local, (q_raw, w_gu, scale_b, scale_d, a_parts, b_parts, ad_parts, bd_parts) = arena(
                ("q_raw", [P, 3, I_FFN], I32), ("w_gu", [P, NK, 2, I_FFN], F32), ("scale_b", [P, 2, I_FFN], F32),
                ("scale_d", [P, D], F32), ("a_parts", [3 * RANK, 2, D], F32R),
                ("b_parts", [3 * RANK, 2, I_FFN], F32R), ("ad_parts", [3 * RANK, I_FFN], F32R),
                ("bd_parts", [3 * RANK, D], F32R))
            def part(buffer, o, shape):
                n = shape[0] * shape[1]
                v = buffer[0:3 * RANK, o:o + n]
                return v.rearrange("r (g c) -> r g c", g=shape[0])

            gu_flat = w_gu[:].rearrange("p k g n -> p (k g n)")
            a_raw = part(gu_flat, 4 * I_FFN, (2, D))
            b_raw = part(gu_flat, 4 * I_FFN + 2 * D, (2, I_FFN))
            x_room = x[:, NT * D:]
            w_raw = x_room[:, 0:NK * 3 * D].rearrange("p (k n) -> p k n", k=NK)
            down_ring = wo
            ad_raw = part(gu_flat, 4 * I_FFN + 2 * D + 2 * I_FFN, (1, I_FFN))
            bd_raw = down_ring[0:3 * RANK, 2, :]

            x_in = sem("x_loaded")
            scales_in = sem("scales_loaded")
            q_in = [sem(f"q_loaded_{i}") for i in range(3)]
            lr_in = [sem(f"lowrank_loaded_{i}") for i in range(3)]
            lr_hi = sem("lowrank_hi")
            lr_lo = sem("lowrank_parts")
            qkv_in = sem("qkv_loaded")
            made = sem("identity_zeroed")
            ident_made = sem("identity_made")
            scaled = sem("scales_ready")
            deq = sem("dequantised")
            shifted = sem("down_shifted")
            deq_down = sem("down_dequantised")
            in_place = sem("weights_scaled_in_place")
            ab = sem("lowrank_product")
            summed = sem("weights_summed")
            maxed = sem("chunk_max_ready")
            allmax = sem("all_reduced")
            stat = sem("weight_scale_steps")
            hi = sem("weight_hi")
            lo = sem("weight_lo")
            lo_pool = sem("weight_lo_pool")
            padded = sem("pads_zeroed")
            down_stored = [sem(f"down_stored_{i}") for i in range(3)]
            qkv_maxed = sem("qkv_max")
            qkv_allmax = sem("qkv_all_reduced")
            qkv_stat = sem("qkv_scale_steps")
            qkv_h = sem("qkv_hi_done")
            qkv_l = sem("qkv_lo_done")
            NQ = 2 * NK
            pieces = [(0, 512), (512, 512), (1024, I_FFN - 1024)]
            ab_units = [(g, k, p) for g in range(2) for k in range(NK) for p in range(3)]
            base = len(ab_units)

            FINISH = [("gu", 0, (0,), ()), ("gu", 1, (1,), ()), ("gu", 2, (2,), ()), ("qkv", 0, (), (3,)),
                      ("qkv", 1, (3,), (4,)), ("qkv", 2, (4,), (5,)), ("qkv", 3, range(5, NC), range(6, NC))]

            def down_rows(n):
                return min(P, I_FFN - n * P)

            def ring(c):
                return c % 3 if c < NC - 1 else 3

            with nc.Block() as block:
                @block.sync
                def _(sp):
                    for n in range(NQ):
                        if n == 1:
                            sp.wait_ge(lr_in[0], 96)
                        if n >= 3:
                            sp.wait_ge(deq, n - 2)
                        sp.dma_start(q_raw[:, n % 3, :], rows(a["gate_q_t" if n < NK else "up_q_t"])[:, n % NK, :])\
                            .then_inc(q_in[n % 3], 16)
                    sp.dma_start(w_raw, rows(a["Wqkv_t"])).then_inc(qkv_in, 16)
                    def store(c):
                        sp.wait_ge(summed, base + c + 1)
                        sp.dma_start(down_dram[:, c, :], down_ring[:, ring(c), :]).then_inc(down_stored[c % 3], 16)

                    for c in range(NC):
                        n, r = NQ + c, down_rows(c)
                        if c < 3:
                            sp.wait_ge(deq, n - 2)
                        else:
                            sp.wait_ge(shifted, c - 2)
                        sp.dma_start(q_raw[0:r, n % 3, 0:D], a["down_q_t"][c * P:c * P + r, :])\
                            .then_inc(q_in[n % 3], 16)
                        if c == 2:
                            sp.dma_start(x[:, 0:NT * D].rearrange("p (t d) -> p t d", d=D),
                                         a["x"].rearrange("(t p) d -> p t d", p=P)[:, 0:NT, :]).then_inc(x_in, 16)
                        if c >= 2:
                            store(c - 2)
                    store(NC - 2)
                    store(NC - 1)
                    sp.wait_ge(x_in, 16)
                    for i in range(3):
                        sp.wait_ge(down_stored[i], 16 * len(range(i, NC, 3)))

                @block.gpsimd
                def _(pool):
                    pool.memset(minus_half[:], -0.5).then_inc(made, 1)
                    pool.wait_ge(made, 1)
                    pool.memset(ident[:], 0.0).then_inc(made, 1)
                    pool.wait_ge(made, 2)
                    pool.affine_select(out=ident[:], in_=ident[:], compare_op=ALU.not_equal, fill=1.0, base=0,
                                       pattern=[[-1, P]], channel_multiplier=1).then_inc(ident_made, 1)
                    pool.wait_ge(ident_made, 1)
                    second, third = slice(RANK, 2 * RANK), slice(2 * RANK, 3 * RANK)
                    factors = []
                    for g in range(2):
                        factors += [(a_parts[second, g, :], a_raw[second, g, :]),
                                    (b_parts[third, g, :], b_raw[third, g, :])]
                    factors += [(ad_parts[second, :], ad_raw[second, 0, :]), (bd_parts[third, :], bd_raw[third, :])]
                    for m, (parts, raw) in enumerate(factors):
                        if m >= 1:
                            pool.wait_ge(lr_lo, m)
                        pool.wait_ge(lr_hi, m + 1)
                        pool.tensor_tensor(parts, raw, parts.bitcast(F32), ALU.subtract).then_inc(lr_lo, 1)
                    pool.wait_ge(lr_lo, 6)
                    def dequantise_down(c):
                        pool.wait_ge(shifted, c + 1)
                        ring_c = down_ring[0:down_rows(c), ring(c), :]
                        pool.tensor_tensor(ring_c, ring_c, scale_d[0:down_rows(c), :], ALU.mult).then_inc(deq_down, 1)

                    pool.memset(gu_hi[:, :, :, I_FFN:IP], 0.0).then_inc(padded, 1)
                    pool.memset(gu_lo[:, :, :, I_FFN:IP], 0.0).then_inc(padded, 1)
                    pool.wait_ge(padded, 2)
                    pool.memset(down_ring[down_rows(NC - 1):P, 3, :], 0.0).then_inc(padded, 1)
                    pool.wait_ge(padded, 3)
                    pool.wait_ge(scaled, 3)
                    for c in range(2):
                        dequantise_down(c)
                        pool.wait_ge(deq_down, c + 1)
                    pool.wait_ge(stat, 1)
                    pool.partition_all_reduce(gmax, rmax, P, RMAX).then_inc(allmax, 1)
                    pool.wait_ge(qkv_stat, 1)
                    pool.partition_all_reduce(gmax, rmax, P, RMAX).then_inc(qkv_allmax, 1)
                    pool.wait_ge(qkv_allmax, 1)
                    pool.wait_ge(in_place, 1)
                    pool.tensor_tensor(gu_lo[:, NK - 1, :, 0:I_FFN], w_gu[:, NK - 1, :, :],
                                       gu_hi[:, NK - 1, :, 0:I_FFN], ALU.subtract).then_inc(lo_pool, 1)
                    pool.wait_ge(lo_pool, 1)
                    for c in range(2, NC):
                        dequantise_down(c)
                        pool.wait_ge(deq_down, c + 1)

                @block.tensor
                def _(pe):
                    for n, (g, k, p) in enumerate(ab_units):
                        o, w = pieces[p]
                        if k == 0 and p == 0:
                            pe.wait_ge(lr_lo, 2 * g + 2)
                        if n >= 8:
                            pe.wait_ge(summed, n - 7)
                        pe.matmul(bank[n % 8][:, 0:w], a_parts[:, g, k * P:(k + 1) * P], b_parts[:, g, o:o + w],
                                  start=True, stop=True).then_inc(ab, 1)
                    pe.wait_ge(lr_lo, 6)
                    for c in range(NC):
                        r = down_rows(c)
                        pe.wait_ge(summed, base + c - 7)
                        pe.matmul(bank[(base + c) % 8][0:r, :], ad_parts[:, c * P:c * P + r], bd_parts[:],
                                  start=True, stop=True).then_inc(ab, 1)

                @block.scalar
                def _(act):
                    for g, w in enumerate(("gate", "up")):
                        for m in range(3):
                            rs = slice(m * RANK, (m + 1) * RANK)
                            act.dma_start(a_raw[rs, g, :], a[w + "_A_t"]).then_inc(lr_in[g], 16)
                            act.dma_start(b_raw[rs, g, :], a[w + "_B"]).then_inc(lr_in[g], 16)
                        act.dma_start(scale_b[:, g, :], bcast(a[w + "_scale"])).then_inc(scales_in, 16)
                    act.dma_start(scale_d[:], bcast(a["down_scale"])).then_inc(scales_in, 16)
                    for m in range(3):
                        rs = slice(m * RANK, (m + 1) * RANK)
                        act.dma_start(ad_raw[rs, 0, :], a["down_A_t"]).then_inc(lr_in[2], 16)
                        act.dma_start(bd_raw[rs, :], a["down_B"]).then_inc(lr_in[2], 16)
                    for g in range(2):
                        act.wait_ge(lr_in[g], 96)
                        act.copy(a_parts[:, g, :], a_raw[:, g, :]).then_inc(lr_hi, 1)
                        act.copy(b_parts[:, g, :], b_raw[:, g, :]).then_inc(lr_hi, 1)
                    act.wait_ge(lr_in[2], 96)
                    act.copy(ad_parts[:], ad_raw[:, 0, :]).then_inc(lr_hi, 1)
                    act.copy(bd_parts[:], bd_raw).then_inc(lr_hi, 1)
                    def shift_down(c):
                        if 3 <= c < NC - 1:
                            act.wait_ge(down_stored[c % 3], 16 * (c // 3))
                        act.wait_ge(q_in[(NQ + c) % 3], 16 * ((NQ + c) // 3 + 1))
                        act.activation(down_ring[0:down_rows(c), ring(c), :],
                                       q_raw[0:down_rows(c), (NQ + c) % 3, 0:D], ACT.Copy, bias=-Q_ZERO)\
                            .then_inc(shifted, 1)

                    def scale_high(k):
                        act.activation(gu_hi[:, k, :, 0:I_FFN], w_gu[:, k, :, :], ACT.Copy, scale=w_gu_scale)\
                            .then_inc(hi, 1)

                    act.wait_ge(lr_lo, 6)
                    act.wait_ge(padded, 3)
                    for c in range(3):
                        shift_down(c)
                    act.wait_ge(stat, 5)
                    scale_high(NK - 1)
                    act.wait_ge(hi, 1)
                    act.activation(w_gu[:, NK - 1, :, :], w_gu[:, NK - 1, :, :], ACT.Copy, scale=w_gu_scale)\
                        .then_inc(in_place, 1)
                    for what, k, _, chunks in FINISH:
                        if what == "gu":
                            scale_high(k)
                        else:
                            act.wait_ge(qkv_stat, 5)
                            act.activation(qkv_hi[:, k, :], w_raw[:, k, :], ACT.Copy, scale=wsc).then_inc(qkv_h, 1)
                        for c in chunks:
                            shift_down(c)

                @block.vector
                def _(dve):
                    def low(k):
                        dve.scalar_tensor_tensor(out=gu_lo[:, k, :, 0:I_FFN], in0=w_gu[:, k, :, :],
                                                 scalar=w_gu_scale, in1=gu_hi[:, k, :, 0:I_FFN],
                                                 op0=ALU.mult, op1=ALU.subtract).then_inc(lo, 1)

                    dve.wait_ge(scales_in, 48)
                    for g in range(2):
                        dve.tensor_scalar(scale_b[:, g, :], scale_b[:, g, :], Q_STEP, None, ALU.mult)\
                            .then_inc(scaled, 1)
                    dve.tensor_scalar(scale_d[:], scale_d[:], Q_STEP, None, ALU.mult).then_inc(scaled, 1)
                    dve.wait_ge(scaled, 3)
                    for n in range(NQ):
                        g, k = n // NK, n % NK
                        dve.wait_ge(q_in[n % 3], 16 * (n // 3 + 1))
                        if n == 2:
                            dve.wait_ge(lr_lo, 5)
                        dve.scalar_tensor_tensor(out=w_gu[:, k, g, :], in0=q_raw[:, n % 3, :],
                                                 scalar=-Q_ZERO, in1=scale_b[:, g, :],
                                                 op0=ALU.add, op1=ALU.mult).then_inc(deq, 1)
                        dve.wait_ge(deq, n + 1)
                        for p, (o, w) in enumerate(pieces):
                            m = 3 * n + p
                            dve.wait_ge(ab, m + 1)
                            dve.scalar_tensor_tensor(out=w_gu[:, k, g, o:o + w], in0=bank[m % 8][:, 0:w],
                                                     scalar=LR_SCALE, in1=w_gu[:, k, g, o:o + w],
                                                     op0=ALU.mult, op1=ALU.add).then_inc(summed, 1)
                        dve.wait_ge(summed, 3 * n + 3)
                        dve.tensor_reduce(chunk_max[:, n:n + 1], w_gu[:, k, g, :], AX.X, ALU.max,
                                          apply_absolute_value=True).then_inc(maxed, 1)
                    dve.wait_ge(maxed, NQ)
                    weight_scale(dve, NQ, c_gu[:], stat, allmax, w_gu_scale)
                    dve.wait_ge(qkv_in, 16)
                    for k in range(NK):
                        dve.tensor_reduce(chunk_max[:, k:k + 1], w_raw[:, k, :], AX.X, ALU.max,
                                          apply_absolute_value=True).then_inc(qkv_maxed, 1)
                    dve.wait_ge(qkv_maxed, NK)
                    weight_scale(dve, NK, c_qkv, qkv_stat, qkv_allmax, wsc)
                    dve.tensor_scalar(c_q, c_qkv, HD ** -0.5, None, ALU.mult).then_inc(qkv_stat, 1)
                    for what, k, chunks, _ in FINISH:
                        if what == "gu":
                            dve.wait_ge(hi, k + 2)
                            low(k)
                        else:
                            dve.wait_ge(qkv_h, k + 1)
                            dve.scalar_tensor_tensor(out=qkv_lo[:, k, :], in0=w_raw[:, k, :], scalar=wsc,
                                                     in1=qkv_hi[:, k, :], op0=ALU.mult, op1=ALU.subtract)\
                                .then_inc(qkv_l, 1)
                        for c in chunks:
                            r = down_rows(c)
                            dve.wait_ge(deq_down, c + 1)
                            dve.wait_ge(ab, base + c + 1)
                            dve.scalar_tensor_tensor(out=down_ring[0:r, ring(c), :],
                                                     in0=bank[(base + c) % 8][0:r, :], scalar=LR_SCALE,
                                                     in1=down_ring[0:r, ring(c), :],
                                                     op0=ALU.mult, op1=ALU.add).then_inc(summed, 1)
                    dve.wait_ge(qkv_l, NK)
                    dve.wait_ge(lo, NK - 1)
                    dve.wait_ge(qkv_stat, 6)
            local.close()
            end_phase()

        def weight_scale(dve, n, undo, stat, allmax, scale):
            dve.tensor_reduce(rmax, chunk_max[:, 0:n], AX.X, ALU.max).then_inc(stat, 1)
            dve.wait_ge(allmax, 1)
            dve.tensor_scalar(gmax, gmax, 1e-30, None, ALU.max).then_inc(stat, 1)
            dve.wait_ge(stat, 2)
            dve.reciprocal(scale, gmax).then_inc(stat, 1)
            dve.tensor_scalar(undo, gmax, 1.0 / (W_TOP * X_SCALE), None, ALU.mult).then_inc(stat, 1)
            dve.wait_ge(stat, 4)
            dve.tensor_scalar(scale, scale, W_TOP, None, ALU.mult).then_inc(stat, 1)
            dve.wait_ge(stat, 5)

        class Norm:

            def __init__(self, xn, x_hi, x_lo, stats):
                self.xn, self.x_hi, self.x_lo = xn, x_hi, x_lo
                self.raw = stats[:, 0:24].rearrange("p (i s) -> p i s", s=6)
                self.mv = stats[:, 24:32].rearrange("p (i s) -> p i s", s=2)
                self.var = stats[:, 32:36]
                self.rstd = stats[:, 36:40]
                self.stats = sem("bn_stats")
                self.aggr = sem("bn_aggr")
                self.eps = sem("eps_added")
                self.inv = sem("rstd_ready")
                self.xn_ready = sem("xn_ready")
                self.turned = sem("xn_turned")
                self.hi_done = sem("x_hi_done")
                self.lo_done = sem("x_lo_done")

            def take_stats(self, dve, b, i):
                dve.bn_stats(self.raw[:, i, :], x[:, bass.ds((b * NT + i) * D, D)]).then_inc(self.stats, 1)

            def aggregate(self, dve, b):
                hold(dve, self.stats, b * NT + NT)
                for i in range(NT):
                    dve.bn_aggr(self.mv[:, i, :], self.raw[:, i, :]).then_inc(self.aggr, 1)
                dve.wait_ge(self.aggr, b * NT + NT)
                dve.tensor_scalar(self.var, self.mv[:, :, 1], EPS, None, ALU.add).then_inc(self.eps, 1)

            def scale(self, dve, b, i):
                if i == 0:
                    dve.wait_ge(self.inv, b + 1)
                dve.tensor_scalar(self.xn[:, i, :], x[:, bass.ds((b * NT + i) * D, D)], self.mv[:, i, 0:1],
                                  self.rstd[:, i:i + 1], ALU.subtract, ALU.mult).then_inc(self.xn_ready, 1)

            def normalise(self, dve, b):
                for i in range(NT):
                    self.take_stats(dve, b, i)
                self.aggregate(dve, b)
                for i in range(NT):
                    self.scale(dve, b, i)

            def invert(self, pool, b):
                pool.wait_ge(self.eps, b + 1)
                pool.tensor_tensor(self.rstd, self.var, minus_half[:, 0:NT], ALU.pow).then_inc(self.inv, 1)

            def low(self, dve, b, k, src):
                dve.wait_ge(self.hi_done, b * NK + k + 1)
                dve.scalar_tensor_tensor(out=self.x_lo[:, k, :], in0=src[:], scalar=X_SCALE,
                                         in1=self.x_hi[:, k, :], op0=ALU.mult, op1=ALU.subtract)\
                    .then_inc(self.lo_done, 1)

            def high(self, act, b, k, src):
                act.wait_ge(self.turned, b * NK + k + 1)
                act.activation(self.x_hi[:, k, :], src[:], ACT.Copy, scale=X_SCALE).then_inc(self.hi_done, 1)

            def turn(self, pe, b, k, dst):
                pe.wait_ge(self.xn_ready, b * NT + NT)
                for i in range(NT):
                    t = pe.transpose(dst[:, i * P:(i + 1) * P], self.xn[:, i, k * P:(k + 1) * P], ident[:])
                t.then_inc(self.turned, 1)

        def attention(is_b, w_out, masks, lnw, slopes, bias_out, broadcasts):
            GROUPS = H // HPB
            PAIRS = HPB // 2
            UPB = HPB * UPH
            UPP = 2 * UPH
            TRI = NT * (NT + 1) // 2 * P
            local, (qkv, v_parts, split_q, split_k, q_t, k_t, s_buf, p_hi, p_lo, head_bias, x_hi, x_lo,
                    xn, attn, stats) = arena(
                ("qk", [P, 2, NT, D], F32), ("v_parts", [P, NT, H, VW], BF16),
                ("split_q", [P, NT, P], F32R), ("split_k", [P, NT, P], F32R),
                ("q_t", [P, 2, S], F32R), ("k_t", [P, 2, S], F32R),
                ("s_buf", [P, TRI], F32), ("p_hi", [P, TRI], F16), ("p_lo", [P, TRI], F16),
                ("head_bias", [P, HPB, S], F32), ("x_hi", [P, NK, S], F16), ("x_lo", [P, NK, S], F16),
                ("xn", [P, NT, D], F32), ("attn", [P, NT, D], F32),
                ("stats", [P, 144], F32))
            tmp = head_bias[:, 2:4]
            norm = Norm(xn, x_hi, x_lo, stats)
            neg_max = stats[:, 40:44]
            rsum = stats[:, 44:52]
            q_raw = stats[:, 52:100].rearrange("p (i s) -> p i s", s=6)
            q_mv = stats[:, 100:116].rearrange("p (i s) -> p i s", s=2)
            q_var = stats[:, 116:124]
            q_rstd = stats[:, 124:132]

            wo_in = sem("wo_loaded")
            rows_in = sem("broadcasts_loaded")
            x_in = sem("x_rest_loaded")
            mask_step = sem("mask_step")
            row_scaled = sem("broadcasts_scaled")
            proj = sem("projected")
            evac = sem("qkv_bank_read")
            q_fixed = sem("qk_clipped")
            q_stats = sem("qk_bn_stats")
            q_aggr = sem("qk_bn_aggr")
            q_eps = sem("qk_eps")
            q_inv = sem("qk_rstd")
            q_norm = sem("qk_normed")
            q_gain = sem("qk_gained_pool")
            q_done = sem("qk_final_pool")
            q_gain_v = sem("qk_gained_vector")
            q_done_v = sem("qk_final_vector")
            v_ready = sem("v_ready")
            v_h = sem("v_high")
            v_r = sem("v_rest")
            v_m = sem("v_middle")
            v_l = sem("v_low")
            ones = sem("ones_set")
            sp_hi = sem("split_hi")
            sp_lo = sem("split_lo")
            bias_ready = sem("head_bias_ready")
            qk_turned = sem("qk_turned")
            qk_t_ready = sem("qk_t_ready")
            s_ready = sem("scores_ready")
            s_masked = sem("scores_masked")
            p_ready = sem("probs_ready")
            p_turned = sem("probs_turned")
            hi_ready = sem("probs_hi")
            lo_ready = sem("probs_lo")
            pv_done = sem("values_product")
            pv_sum = sem("pair_summed")
            r_ready = sem("rsum_ready")
            o_ready = sem("pair_out")
            o_turned = sem("o_turned")
            o_t_ready = sem("o_t_ready")
            out_ready = sem("out_ready")
            x_added = sem("x_added")
            bo_added = sem("bo_added")

            FREE = {s_masked: UPB, lo_ready: 3, p_turned: 3, pv_done: 3, pv_sum: 4, qk_t_ready: 2, qk_turned: 2}

            def wait(engine, semaphore, count):
                engine.wait_ge(semaphore, count + FREE.get(semaphore, 0))

            def tile(n):
                return NT - 1 - n % UPH

            def span(n):
                i = tile(n)
                return slice(i * (i + 1) // 2 * P, (i + 1) * (i + 2) // 2 * P)

            P_BANKS = (bank[2], bank[3], bank[4])
            PV_BANKS = (bank[5], bank[6])
            TURN_BANK = bank[7]
            BLOCKS = ((0,), (1,), (2, 3))

            def is_block(n):
                return n % UPH in (0, 1, 3)

            def block_of(b, hg, n):
                return ((b * GROUPS + hg) * HPB + n // UPH) * 3 + (0, 1, None, 2)[n % UPH]

            def block_bank(n):
                return P_BANKS[(0, 1, None, 2)[n % UPH]]

            def block_units(n):
                return [n // UPH * UPH + u for u in BLOCKS[(0, 1, None, 2)[n % UPH]]]

            def block_span(n):
                return slice(min(span(u).start for u in block_units(n)), max(span(u).stop for u in block_units(n)))

            def turned_probs(n):
                return block_bank(n)[:, 0:block_span(n).stop - block_span(n).start]

            T_LAG, HI_LAG, LO_LAG, V_LAG = 1, 3, 5, 6
            TURN_STEPS = (0, 4)
            OUT_STEP = 6
            STATS_STEPS, SCALE_STEPS, NORM_STEPS = (0, 1, 2, 3), (4, 5, 6, 7), (8, 10, 12, 14)
            UNITS = [(0, 0), (0, 1), (1, 0), (1, 1), (0, 2), (2, 0), (2, 1), (1, 2), (3, 0), (3, 1), (2, 2), (3, 2)]
            UNIT_BANKS = (bank[0], bank[1], bank[7], bank[2], bank[3], bank[4])
            O_TURN_BANK, OUT_BANK = bank[5], bank[6]
            BETWEEN = [("v", 0), ("out", 0), ("qk", 2), ("v", 1), ("out", 1), ("qk", 3), ("v", 2), ("out", 2),
                       ("v", 3), ("out", 3)]

            def unit_bank(u):
                return UNIT_BANKS[u % len(UNIT_BANKS)]

            with nc.Block() as block:
                @block.sync
                def _(sp):
                    for dst, src, _ in broadcasts:
                        sp.dma_start(dst, bcast(src)).then_inc(rows_in, 16)
                    if not is_b:
                        sp.dma_start(x[:, NT * D:].rearrange("p (t d) -> p t d", d=D),
                                     a["x"].rearrange("(t p) d -> p t d", p=P)[:, NT:, :]).then_inc(x_in, 16)
                    sp.dma_start(wo[:], rows(w_out)).then_inc(wo_in, 16)

                @block.tensor
                def _(pe):
                    def project(b, u):
                        i, g = UNITS[u]
                        if u == 0:
                            pe.wait_ge(norm.lo_done, b * NK + NK)
                        if u >= len(UNIT_BANKS):
                            pe.wait_ge(evac, b * 12 + u + 1 - len(UNIT_BANKS))
                        n = 0
                        for k in range(NK):
                            for xs, ws in ((x_hi, qkv_hi), (x_lo, qkv_hi), (x_hi, qkv_lo)):
                                t = pe.matmul(unit_bank(u)[:], xs[:, k, i * P:(i + 1) * P],
                                              ws[:, k, g * D:(g + 1) * D], start=(n == 0), stop=(n == 3 * NK - 1))
                                n += 1
                        t.then_inc(proj, 1)

                    def turn_pair(b, hg, pp, g):
                        pair = (b * GROUPS + hg) * PAIRS + pp
                        pe.wait_ge(sp_lo, 2 * pair + g + 1)
                        wait(pe, qk_t_ready, 2 * pair + g)
                        for i in range(NT):
                            t = pe.transpose(TURN_BANK[:, i * P:(i + 1) * P],
                                             (split_q, split_k)[g][:, i, :].bitcast(F32), ident[:])
                        t.then_inc(qk_turned, 1)

                    def scores(b, hg, n):
                        unit = (b * GROUPS + hg) * UPB + n
                        i = tile(n)
                        if n % UPP == 0:
                            pair = (b * GROUPS + hg) * PAIRS + n // UPP
                            wait(pe, qk_t_ready, 2 * pair + 2)
                        wait(pe, s_masked, unit - 1)
                        slot = n // UPP % 2
                        r = 64 * (n // UPH % 2)
                        pe.matmul(bank[n % 2][:, 0:(i + 1) * P], q_t[r:r + 64, slot, i * P:(i + 1) * P],
                                  k_t[r:r + 64, slot, 0:(i + 1) * P], start=True, stop=True).then_inc(s_ready, 1)

                    def turn_probs(b, hg, n):
                        pe.wait_ge(p_ready, (b * GROUPS + hg) * UPB + n + 1)
                        wait(pe, lo_ready, block_of(b, hg, n) - 2)
                        src, dst = s_buf[:, block_span(n)], turned_probs(n)
                        for j in range(dst.shape[1] // P):
                            t = pe.transpose(dst[:, j * P:(j + 1) * P], src[:, j * P:(j + 1) * P], ident[:])
                        t.then_inc(p_turned, 1)

                    def values(b, hg, n):
                        if n % UPP == 0:
                            wait(pe, pv_sum, 2 * ((b * GROUPS + hg) * PAIRS + n // UPP) - 2)
                        wait(pe, lo_ready, block_of(b, hg, n) + 1)
                        for u in block_units(n):
                            i = tile(u)
                            o = (n // UPH % 2 * NT + i) * VW
                            m = 0
                            for j in range(i + 1):
                                for part in (p_hi, p_lo):
                                    t = pe.matmul(PV_BANKS[n // UPP % 2][:, o:o + VW],
                                                  part[:, span(u)][:, j * P:(j + 1) * P],
                                                  v_parts[:, j, bass.ds(hg * HPB + n // UPH, 1), :],
                                                  start=(m == 0), stop=(m == 2 * i + 1))
                                    m += 1
                        t.then_inc(pv_done, 1)

                    def group(b, hg, first=False, last=False, prefetch=False):
                        if first:
                            pe.wait_ge(evac, b * 12 + 12)
                            turn_pair(b, hg, 0, 1)
                            scores(b, hg, 0)
                            scores(b, hg, 1)
                        for n in range(UPB):
                            if n % UPP in TURN_STEPS and not (last and n + UPP >= UPB):
                                turn_pair(b, hg, n // UPP + 1, TURN_STEPS.index(n % UPP))
                            if n + 2 < UPB or not last:
                                scores(b, hg, n + 2)
                            if first and n == V_LAG:
                                hold(pe, v_l, b * NT + NT)
                            if is_block(n - V_LAG) and (n >= V_LAG or not first):
                                values(b, hg, n - V_LAG)
                            if is_block(n - T_LAG) and (n >= T_LAG or not first):
                                turn_probs(b, hg, n - T_LAG)
                            if prefetch and n in NORM_STEPS:
                                k = NORM_STEPS.index(n)
                                if k >= 1:
                                    pe.wait_ge(norm.lo_done, (b + 1) * NK + k)
                                norm.turn(pe, b + 1, k, TURN_BANK)
                        if last:
                            for n in range(UPB, UPB + V_LAG):
                                if is_block(n - V_LAG):
                                    values(b, hg, n - V_LAG)
                                if n < UPB + T_LAG and is_block(n - T_LAG):
                                    turn_probs(b, hg, n - T_LAG)
                                if prefetch and n in (UPB, UPB + 2):
                                    project(b + 1, (n - UPB) // 2)

                    def turn_out(b, i):
                        if i == 0:
                            pe.wait_ge(o_ready, (b + 1) * (H // 2))
                        for k in range(NK):
                            t = pe.transpose(O_TURN_BANK[:, k * P:(k + 1) * P], attn[:, i, k * P:(k + 1) * P],
                                             ident[:])
                        t.then_inc(o_turned, 1)

                    def output(b, i):
                        pe.wait_ge(o_t_ready, b * NT + i + 1)
                        if i + 1 < NT:
                            turn_out(b, i + 1)
                        if i >= 1:
                            pe.wait_ge(x_added, b * NT + i)
                        for k in range(NK):
                            t = pe.matmul(OUT_BANK[:], s_buf[:, i % 2 * D + k * P:i % 2 * D + (k + 1) * P],
                                          wo[:, k, :], start=(k == 0), stop=(k == NK - 1))
                        t.then_inc(out_ready, 1)

                    def turn_first_q(b):
                        pe.wait_ge(evac, b * 12 + 9)
                        turn_pair(b, 0, 0, 0)

                    def heads(b, prefetch):
                        group(b, 0, first=True)
                        with pe.Fori(1, GROUPS - 1) as hg:
                            group(b, hg)
                        group(b, GROUPS - 1, last=True, prefetch=prefetch)

                    for k in range(NK):
                        norm.turn(pe, 0, k, bank[4 + k])
                    for u in range(len(UNITS)):
                        project(0, u)
                    turn_first_q(0)
                    hold(pe, wo_in, 16)
                    with pe.Fori(0, B - 1) as b:
                        heads(b, True)
                        project(b + 1, 2)
                        turn_out(b, 0)
                        project(b + 1, 3)
                        for what, i in BETWEEN:
                            if what == "out":
                                if i == NT - 1:
                                    turn_first_q(b + 1)
                                output(b, i)
                            else:
                                for g in ((0, 1) if what == "qk" else (2,)):
                                    project(b + 1, UNITS.index((i, g)))
                    heads(B - 1, False)
                    turn_out(B - 1, 0)
                    for i in range(NT):
                        output(B - 1, i)

                @block.scalar
                def _(act):
                    def evacuate(b, u, dst):
                        act.wait_ge(proj, b * 12 + u + 1)
                        act.activation(dst, unit_bank(u)[:], ACT.Copy, scale=c_qkv).then_inc(evac, 1)

                    def values_of(b, i, between=None):
                        if not is_b:
                            if i >= 1:
                                act.wait_ge(v_l, b * NT + i)
                            evacuate(b, UNITS.index((i, 2)), tmp[:, 0, :])
                        vv = v_parts[:, i, :, :]
                        act.wait_ge(v_ready, b * NT + i + 1)
                        act.copy(vv[:, :, 0:HD], tmp[:, 0, :].rearrange("p (h d) -> p h d", d=HD)).then_inc(v_h, 1)
                        act.wait_ge(v_r, b * NT + i + 1)
                        act.copy(vv[:, :, HD:2 * HD], tmp[:, 1, :].rearrange("p (h d) -> p h d", d=HD))\
                            .then_inc(v_m, 1)

                    def copy_pair(b, hg, pp, g):
                        pair = (b * GROUPS + hg) * PAIRS + pp
                        wait(act, qk_turned, 2 * pair + g + 1)
                        act.copy((q_t, k_t)[g][:, pp % 2, :], TURN_BANK[:]).then_inc(qk_t_ready, 1)

                    def exps(b, hg, n):
                        unit = (b * GROUPS + hg) * UPB + n
                        wait(act, s_masked, unit + 1)
                        act.activation(s_buf[:, span(n)], s_buf[:, span(n)], ACT.Exp,
                                       bias=neg_max[:, n % 4:n % 4 + 1], scale=-1.0).then_inc(p_ready, 1)

                    def highs(b, hg, n):
                        wait(act, p_turned, block_of(b, hg, n) + 1)
                        wait(act, pv_done, block_of(b, hg, n) - 2)
                        act.copy(p_hi[:, block_span(n)], turned_probs(n)).then_inc(hi_ready, 1)

                    def group(b, hg, first=False, last=False, prefetch=False):
                        if first:
                            copy_pair(b, hg, 0, 0)
                            copy_pair(b, hg, 0, 1)
                        for n in range(UPB):
                            exps(b, hg, n)
                            if is_block(n - HI_LAG) and (n >= HI_LAG or not first):
                                highs(b, hg, n - HI_LAG)
                            if n % UPP in TURN_STEPS and not (last and n + UPP >= UPB):
                                copy_pair(b, hg, n // UPP + 1, TURN_STEPS.index(n % UPP))
                            if prefetch and n in NORM_STEPS:
                                norm.high(act, b + 1, NORM_STEPS.index(n), TURN_BANK)
                        if last:
                            for n in range(UPB - HI_LAG, UPB):
                                if is_block(n):
                                    highs(b, hg, n)

                    def copy_out(b, i):
                        act.wait_ge(o_turned, b * NT + i + 1)
                        act.copy(s_buf[:, i % 2 * D:(i % 2 + 1) * D], O_TURN_BANK[:]).then_inc(o_t_ready, 1)

                    def heads(b, prefetch):
                        group(b, 0, first=True)
                        with act.Fori(1, GROUPS - 1) as hg:
                            group(b, hg)
                        group(b, GROUPS - 1, last=True, prefetch=prefetch)

                    def evacuate_qk(b, i):
                        for g in range(2):
                            if not is_b:
                                evacuate(b, UNITS.index((i, g)), qkv[:, g, i, :])

                    def between(b, out=True):
                        evacuate_qk(b + 1, 0)
                        evacuate_qk(b + 1, 1)
                        if out:
                            copy_out(b, 0)
                        for what, i in BETWEEN:
                            if what == "qk":
                                evacuate_qk(b + 1, i)
                            elif what == "v":
                                values_of(b + 1, i)
                            elif out and i + 1 < NT:
                                copy_out(b, i + 1)

                    for k in range(NK):
                        norm.high(act, 0, k, bank[4 + k])
                    between(-1, out=False)
                    with act.Fori(0, B - 1) as b:
                        heads(b, True)
                        between(b)
                    heads(B - 1, False)
                    for i in range(NT):
                        copy_out(B - 1, i)

                @block.vector
                def _(dve):
                    for semaphore, count in FREE.items():
                        dve.sem_inc(semaphore, count)

                    def qk_normalise(b, i):
                        dve.wait_ge(q_inv, b * NT + i + 1)
                        for g in range(2):
                            n = 2 * i + g
                            dve.tensor_scalar(qkv[:, g, i, :], qkv[:, g, i, :], q_mv[:, n, 0:1],
                                              q_rstd[:, n:n + 1], ALU.subtract, ALU.mult).then_inc(q_norm, 1)

                    def finish_qk(b, i):
                        for g in range(2):
                            u, m = UNITS.index((i, g)), 2 * i + g
                            dst = qkv[:, g, i, :]
                            if is_b:
                                dve.wait_ge(proj, b * 12 + u + 1)
                                dve.scalar_tensor_tensor(out=dst, in0=unit_bank(u)[:], scalar=(c_q, c_qkv)[g],
                                                         in1=lnw[:, g, :], op0=ALU.mult, op1=ALU.add)\
                                    .then_inc(evac, 1)
                                continue
                            dve.wait_ge(evac, b * 12 + u + 1)
                            dve.tensor_scalar(dst, dst, CLIP, -CLIP, ALU.min, ALU.max).then_inc(q_fixed, 1)
                            dve.wait_ge(q_fixed, b * 8 + m + 1)
                            dve.bn_stats(q_raw[:, m, :], dst).then_inc(q_stats, 1)
                            if g == 1:
                                hold(dve, q_stats, b * 8 + m + 1)
                                for n in (m - 1, m):
                                    dve.bn_aggr(q_mv[:, n, :], q_raw[:, n, :]).then_inc(q_aggr, 1)
                                dve.wait_ge(q_aggr, b * 8 + m + 1)
                                dve.tensor_scalar(q_var[:, m - 1:m + 1], q_mv[:, m - 1:m + 1, 1],
                                                  EPS, None, ALU.add).then_inc(q_eps, 1)
                                qk_normalise(b, i)
                        if not is_b and i == NT - 1:
                            dve.wait_ge(q_norm, b * 8 + 8)
                            for g in range(2):
                                dve.tensor_tensor(qkv[:, g, i, :], qkv[:, g, i, :], lnw[:, g, :], ALU.mult)\
                                    .then_inc(q_gain_v, 1)
                            for g in range(2):
                                dve.wait_ge(q_gain_v, b * 2 + g + 1)
                                dve.tensor_tensor(qkv[:, g, i, :], qkv[:, g, i, :], lnw[:, 2 + g, :], ALU.add)\
                                    .then_inc(q_done_v, 1)

                    def finish_values(b, i):
                        u = UNITS.index((i, 2))
                        if i >= 1:
                            dve.wait_ge(v_l, b * NT + i)
                        if is_b:
                            dve.wait_ge(proj, b * 12 + u + 1)
                            dve.scalar_tensor_tensor(out=tmp[:, 0, :], in0=unit_bank(u)[:], scalar=c_qkv,
                                                     in1=lnw[:, 2, :], op0=ALU.mult, op1=ALU.add).then_inc(evac, 1)
                            dve.wait_ge(evac, b * 12 + u + 1)
                            dve.sem_inc(v_ready, 1)
                        else:
                            dve.wait_ge(evac, b * 12 + u + 1)
                            dve.tensor_scalar(tmp[:, 0, :], tmp[:, 0, :], CLIP, -CLIP, ALU.min, ALU.max)\
                                .then_inc(v_ready, 1)
                        vv = v_parts[:, i, :, :]
                        t0 = tmp[:, 0, :].rearrange("p (h d) -> p h d", d=HD)
                        t1 = tmp[:, 1, :].rearrange("p (h d) -> p h d", d=HD)
                        dve.wait_ge(v_h, b * NT + i + 1)
                        dve.tensor_tensor(t1, t0, vv[:, :, 0:HD], ALU.subtract).then_inc(v_r, 1)
                        dve.wait_ge(v_m, b * NT + i + 1)
                        dve.tensor_tensor(vv[:, :, 2 * HD:3 * HD], t1, vv[:, :, HD:2 * HD], ALU.subtract)\
                            .then_inc(v_l, 1)

                    def mask_max(b, hg, n):
                        unit = (b * GROUPS + hg) * UPB + n
                        w = (tile(n) + 1) * P
                        if not is_b and n % UPH == 0:
                            dve.wait_ge(bias_ready, (b * GROUPS + hg) * HPB + n // UPH + 1)
                        if n % UPH == 2:
                            wait(dve, p_turned, ((b * GROUPS + hg) * HPB + n // UPH) * 3)
                        hold(dve, s_ready, unit + 1)
                        table = masks[:, S - w:S] if is_b else head_bias[:, n // UPH, S - w:S]
                        dve.tensor_tensor_reduce(out=s_buf[:, span(n)], in0=bank[n % 2][:, 0:w], in1=table,
                                                 scale=-1.0, scalar=BIG, op0=ALU.add, op1=ALU.min,
                                                 accum_out=neg_max[:, n % 4:n % 4 + 1]).then_inc(s_masked, 1)

                    def lows(b, hg, n):
                        dve.wait_ge(hi_ready, block_of(b, hg, n) + 1)
                        cols = block_span(n)
                        dve.tensor_tensor(p_lo[:, cols], turned_probs(n), p_hi[:, cols], ALU.subtract)\
                            .then_inc(lo_ready, 1)

                    def pair_sum(b, hg, pp):
                        wait(dve, pv_done, ((b * GROUPS + hg) * PAIRS + pp + 1) * 6)
                        src = PV_BANKS[pp % 2][:, 0:2 * NT * VW].rearrange("p (i v) -> p i v", v=VW)
                        dve.reciprocal(rsum, src[:, :, 3 * HD]).then_inc(r_ready, 1)
                        parts = src[:, :, 0:3 * HD].rearrange("p (h i) (t c) -> p h i c t", h=2, t=3)
                        for h in range(2):
                            dve.tensor_reduce(attn[:, :, bass.ds((hg * HPB + 2 * pp + h) * HD, HD)],
                                              parts[:, h], AX.X, ALU.add).then_inc(pv_sum, 1)

                    def pair_out(b, hg, pp):
                        pair = (b * GROUPS + hg) * PAIRS + pp
                        dve.wait_ge(r_ready, pair + 1)
                        wait(dve, pv_sum, 2 * pair + 2)
                        cols = attn[:, :, bass.ds((hg * HPB + 2 * pp) * HD, 2 * HD)]\
                            .rearrange("p i (h c) -> p i h c", h=2)
                        rs = rsum.rearrange("p (h i) -> p i h", h=2).unsqueeze(3).to_broadcast([P, NT, 2, HD])
                        dve.tensor_tensor(cols, cols, rs, ALU.mult).then_inc(o_ready, 1)

                    def group(b, hg, first=False, last=False, prefetch=False):
                        for n in range(UPB):
                            mask_max(b, hg, n)
                            if is_block(n - LO_LAG) and (n >= LO_LAG or not first):
                                lows(b, hg, n - LO_LAG)
                            if n >= UPP or not first:
                                if n % UPP == OUT_STEP:
                                    pair_sum(b, hg, n // UPP - 1)
                                if n % UPP == OUT_STEP + 1:
                                    pair_out(b, hg, n // UPP - 1)
                            if prefetch:
                                if n in STATS_STEPS:
                                    norm.take_stats(dve, b + 1, STATS_STEPS.index(n))
                                if n == STATS_STEPS[-1]:
                                    norm.aggregate(dve, b + 1)
                                if n in SCALE_STEPS:
                                    norm.scale(dve, b + 1, SCALE_STEPS.index(n))
                                if n - 1 in NORM_STEPS:
                                    norm.low(dve, b + 1, NORM_STEPS.index(n - 1), TURN_BANK)
                        if last:
                            for n in range(UPB - LO_LAG, UPB):
                                if is_block(n):
                                    lows(b, hg, n)
                            pair_sum(b, hg, PAIRS - 1)
                            pair_out(b, hg, PAIRS - 1)

                    def add_out(b, i):
                        dve.wait_ge(out_ready, b * NT + i + 1)
                        if is_b and i == 0:
                            dve.wait_ge(bo_added, b * NT + NT)
                        xt = x[:, bass.ds((b * NT + i) * D, D)]
                        dve.tensor_tensor(xt, OUT_BANK[:], xt, ALU.add).then_inc(x_added, 1)

                    def heads(b, prefetch):
                        group(b, 0, first=True)
                        with dve.Fori(1, GROUPS - 1) as hg:
                            group(b, hg)
                        group(b, GROUPS - 1, last=True, prefetch=prefetch)

                    norm.normalise(dve, 0)
                    for k in range(NK):
                        norm.low(dve, 0, k, bank[4 + k])
                    dve.wait_ge(rows_in, 16 * len(broadcasts))
                    n = 0
                    for dst, _, factor in broadcasts:
                        if factor != 1.0:
                            dve.tensor_scalar(dst, dst, factor, None, ALU.mult).then_inc(row_scaled, 1)
                            n += 1
                    dve.wait_ge(row_scaled, n)
                    dve.wait_ge(mask_step, 2)
                    if not is_b:
                        dve.wait_ge(x_in, 16)
                    def between(b, out=True):
                        finish_qk(b + 1, 0)
                        finish_qk(b + 1, 1)
                        for what, i in BETWEEN:
                            if what == "qk":
                                finish_qk(b + 1, i)
                            elif what == "v":
                                finish_values(b + 1, i)
                            elif out:
                                add_out(b, i)

                    between(-1, out=False)
                    with dve.Fori(0, B - 1) as b:
                        heads(b, True)
                        between(b)
                    heads(B - 1, False)
                    for i in range(NT):
                        add_out(B - 1, i)

                @block.gpsimd
                def _(pool):
                    if is_b:
                        pool.memset(masks[:], 0.0).then_inc(mask_step, 1)
                    else:
                        pool.iota(masks[:], pattern=[[1, S]], base=-(S - P), channel_multiplier=-1,
                                  allow_small_or_imprecise_dtypes=True).then_inc(mask_step, 1)
                    pool.wait_ge(mask_step, 1)
                    pool.affine_select(out=masks[:], in_=masks[:], compare_op=ALU.is_ge, fill=MASKED,
                                       base=S - P, pattern=[[-1, S]], channel_multiplier=1).then_inc(mask_step, 1)
                    pool.wait_ge(mask_step, 2)
                    for i in range(NT):
                        t = pool.memset(v_parts[:, i, :, 3 * HD:VW], 1.0)
                    t.then_inc(ones, 1)
                    pool.wait_ge(ones, 1)

                    def gain(b, i):
                        pool.wait_ge(q_norm, b * 8 + 2 * i + 2)
                        for g in range(2):
                            pool.tensor_tensor(qkv[:, g, i, :], qkv[:, g, i, :], lnw[:, g, :], ALU.mult)\
                                .then_inc(q_gain, 1)
                        for g in range(2):
                            pool.wait_ge(q_gain, (b * (NT - 1) + i) * 2 + g + 1)
                            pool.tensor_tensor(qkv[:, g, i, :], qkv[:, g, i, :], lnw[:, 2 + g, :], ALU.add)\
                                .then_inc(q_done, 1)

                    def split(b, hg, pp, g):
                        pair = (b * GROUPS + hg) * PAIRS + pp
                        wait(pool, qk_turned, 2 * pair + g - 1)
                        src = qkv[:, g, :, bass.ds((hg * HPB + 2 * pp) * HD, 2 * HD)]\
                            .rearrange("p i (h d) -> p i h d", h=2)
                        to = (split_q, split_k)[g][:].rearrange("p i (h m d) -> p i h m d", h=2, m=4)
                        highs, lows = ((0, 2), (1, 3)) if g == 0 else ((0, 1), (2, 3))
                        for m in highs:
                            t = pool.tensor_copy(to[:, :, :, m, :], src)
                        t.then_inc(sp_hi, 1)
                        hold(pool, sp_hi, 2 * pair + g + 1)
                        for m in lows:
                            t = pool.tensor_tensor(to[:, :, :, m, :], src, to[:, :, :, highs[1], :], ALU.subtract)
                        t.then_inc(sp_lo, 1)

                    def biases_of(b, hg, h):
                        head = (b * GROUPS + hg) * HPB + h
                        hold(pool, s_masked, UPH * (head - HPB + 1) + FREE[s_masked])
                        pool.tensor_tensor(head_bias[:, h, :], masks[:],
                                           slopes[:, bass.ds(hg * HPB + h, 1)].to_broadcast([P, S]), ALU.mult)\
                            .then_inc(bias_ready, 1)

                    def finish_qk(b):
                        norm.invert(pool, b)
                        if is_b:
                            hold(pool, norm.xn_ready, b * NT + NT)
                            for i in range(NT):
                                xt = x[:, bass.ds((b * NT + i) * D, D)]
                                pool.tensor_tensor(xt, xt, bias_out[:], ALU.add).then_inc(bo_added, 1)
                            hold(pool, evac, b * 12 + UNITS.index((NT - 1, 1)) + 1)
                        else:
                            for i in range(NT):
                                hold(pool, q_eps, b * NT + i + 1)
                                pool.tensor_tensor(q_rstd[:, 2 * i:2 * i + 2], q_var[:, 2 * i:2 * i + 2],
                                                   minus_half[:, 0:2], ALU.pow).then_inc(q_inv, 1)
                                if i >= 1:
                                    gain(b, i - 1)
                            pool.wait_ge(q_done, (b + 1) * 2 * (NT - 1))
                            hold(pool, q_done_v, b * 2 + 2)

                    def heads(b):
                        with pool.Fori(0, GROUPS) as hg:
                            for pp in range(PAIRS):
                                for g in range(2):
                                    split(b, hg, pp, g)
                                    if not is_b:
                                        if 2 * pp + g == 2:
                                            hold(pool, v_l, b * NT + NT)
                                        biases_of(b, hg, 2 * pp + g)

                    pool.wait_ge(rows_in, 16 * len(broadcasts))
                    finish_qk(0)
                    with pool.Fori(0, B - 1) as b:
                        heads(b)
                        finish_qk(b + 1)
                    heads(B - 1)
            local.close()
            end_phase()

        def ffn(last_layer, next_weights=()):
            local, (xn, x_hi, x_lo, dn_hi, dn_lo, hid, h_hi, h_lo, stats, w_room) = arena(
                ("xn", [P, NT, D], F32), ("fx_hi", [P, NK, S], F16), ("fx_lo", [P, NK, S], F16),
                ("dn_hi", [P, NC, D], F32R), ("dn_lo", [P, NC, D], F32R),
                ("hid", [P, 2, S], F32),
                ("h_hi", [P, 2, S], F32R), ("h_lo", [P, 2, S], F32R), ("fstats", [P, 48], F32),
                ("w_room", [P, NK * 3 * D], F32))
            norm = Norm(xn[:], x_hi, x_lo, stats)
            down_in = [sem("down_loaded") for _ in range(3)]
            thirds = [range(0, 4), range(4, 8), range(8, NC)]
            PAIRS = (NC - 3) // 2
            w_down = w_room[:, 0:NC * D].rearrange("p (c d) -> p c d", d=D)
            w_raw = w_room[:].rearrange("p (k n) -> p k n", k=NK)
            w_in = sem("next_weights_loaded")
            w_maxed = sem("next_weights_max")
            w_stat = sem("next_weights_scale_steps")
            w_allmax = sem("next_weights_all_reduced")
            w_hi = sem("next_weights_hi")
            w_lo = sem("next_weights_lo")
            assert PAIRS == NK
            dhi = sem("down_hi")
            dlo = sem("down_lo")
            gate_ready = sem("gate_ready")
            up_ready = sem("up_ready")
            sig_ready = sem("silu_ready")
            hid_ready = sem("hidden_ready")
            hhi = sem("hidden_hi")
            hlo = sem("hidden_lo")
            down = sem("down_used")
            x_added = sem("ffn_x_added")
            stored = sem("stored")
            out_v = out.rearrange("(t p) d -> p t d", p=P)
            x_v = x[:].rearrange("p (t d) -> p t d", d=D)
            turn_banks = [bank[6], bank[7], bank[4], bank[5]]

            with nc.Block() as block:
                @block.tensor
                def _(pe):
                    def gate_up(b, c, s):
                        for g in range(2):
                            n = 0
                            for k in range(NK):
                                for ws, xs in ((gu_hi, x_hi), (gu_hi, x_lo), (gu_lo, x_hi)):
                                    t = pe.matmul(bank[4 + 2 * s + g][:], ws[:, k, g, bass.ds(c * P, P)], xs[:, k, :],
                                                  start=(n == 0), stop=(n == 3 * NK - 1))
                                    n += 1
                            t.then_inc(up_ready if g else gate_ready, 1)

                    def contract(b, c, s, first=False, end=False):
                        pe.wait_ge(hlo, b * NC + c + 1)
                        for i in range(NT):
                            for m, (hs, ws) in enumerate(((h_hi, dn_hi), (h_lo, dn_hi), (h_hi, dn_lo))):
                                t = pe.matmul(bank[i][:], hs[:, s, i * P:(i + 1) * P], ws[:, bass.ds(c, 1), :],
                                              start=(first and m == 0), stop=(end and m == 2))
                        t.then_inc(down, 1)

                    def batch(b, begin, more):
                        if begin:
                            for k in range(NK):
                                norm.turn(pe, b, k, turn_banks[k])
                        pe.wait_ge(norm.lo_done, b * NK + NK)
                        gate_up(b, 0, 0)
                        gate_up(b, 1, 1)
                        if not begin:
                            pe.wait_ge(x_added, b * NT)
                        else:
                            pe.wait_ge(dlo, NC)
                        contract(b, 0, 0, first=True)
                        with pe.Fori(0, PAIRS) as j:
                            for s in range(2):
                                c = 2 * j + 2 + s
                                pe.wait_ge(hid_ready, b * NC + c - 1)
                                gate_up(b, c, s)
                                contract(b, c - 1, 1 - s)
                        pe.wait_ge(hid_ready, b * NC + NC - 2)
                        gate_up(b, NC - 1, 0)
                        contract(b, NC - 2, 1)
                        if more:
                            for k in (0, 1):
                                norm.turn(pe, b + 1, k, turn_banks[k])
                            pe.wait_ge(hid_ready, b * NC + NC)
                            for k in (2, 3):
                                norm.turn(pe, b + 1, k, turn_banks[k])
                        contract(b, NC - 1, 0, end=True)

                    batch(0, True, True)
                    with pe.Fori(1, B - 1) as b:
                        batch(b, False, True)
                    batch(B - 1, False, False)

                @block.scalar
                def _(act):
                    def chunk(b, c, s, free=True):
                        act.wait_ge(gate_ready, b * NC + c + 1)
                        act.activation(hid[:, s, :], bank[4 + 2 * s][:], ACT.Silu, scale=c_gu[:]).then_inc(sig_ready, 1)
                        act.wait_ge(hid_ready, b * NC + c + 1)
                        if free:
                            act.wait_ge(down, b * NC + c - 1)
                        act.copy(h_hi[:, s, :], hid[:, s, :]).then_inc(hhi, 1)

                    def batch(b, begin, more):
                        if begin:
                            for k in range(NK):
                                norm.high(act, b, k, turn_banks[k])
                            for third, loaded in zip(thirds, down_in):
                                act.wait_ge(loaded, 16)
                                for c in third:
                                    act.copy(dn_hi[:, c, :], w_down[:, c, :]).then_inc(dhi, 1)
                        chunk(b, 0, 0, free=not begin)
                        chunk(b, 1, 1, free=not begin)
                        with act.Fori(0, PAIRS) as j:
                            for s in range(2):
                                chunk(b, 2 * j + 2 + s, s)
                            if next_weights and not more:
                                act.wait_ge(w_stat, 5)
                                act.activation(qkv_hi[:, bass.ds(j, 1), :], w_raw[:, bass.ds(j, 1), :], ACT.Copy,
                                               scale=wsc).then_inc(w_hi, 1)
                        chunk(b, NC - 1, 0)
                        if more:
                            for k in range(NK):
                                norm.high(act, b + 1, k, turn_banks[k])

                    batch(0, True, True)
                    with act.Fori(1, B - 1) as b:
                        batch(b, False, True)
                    batch(B - 1, False, False)

                @block.vector
                def _(dve):
                    def chunk(b, c, s):
                        dve.wait_ge(sig_ready, b * NC + c + 1)
                        dve.wait_ge(up_ready, b * NC + c + 1)
                        dve.scalar_tensor_tensor(out=hid[:, s, :], in0=bank[5 + 2 * s][:], scalar=c_gu[:],
                                                 in1=hid[:, s, :], op0=ALU.mult, op1=ALU.mult)\
                            .then_inc(hid_ready, 1)
                        dve.wait_ge(hhi, b * NC + c + 1)
                        dve.tensor_tensor(h_lo[:, s, :], hid[:, s, :], h_hi[:, s, :].bitcast(F32), ALU.subtract)\
                            .then_inc(hlo, 1)

                    def batch(b, begin, more):
                        if begin:
                            norm.normalise(dve, b)
                            for k in range(NK):
                                norm.low(dve, b, k, turn_banks[k])
                            for c in range(NC):
                                dve.wait_ge(dhi, c + 1)
                                dve.tensor_tensor(dn_lo[:, c, :], w_down[:, c, :], dn_hi[:, c, :].bitcast(F32),
                                                  ALU.subtract).then_inc(dlo, 1)
                        chunk(b, 0, 0)
                        chunk(b, 1, 1)
                        if more:
                            norm.normalise(dve, b + 1)
                        with dve.Fori(0, PAIRS) as j:
                            for s in range(2):
                                chunk(b, 2 * j + 2 + s, s)
                            if next_weights and begin:
                                dve.wait_ge(w_in, 16 * len(next_weights))
                                dve.tensor_reduce(chunk_max[:, bass.ds(j, 1)], w_raw[:, bass.ds(j, 1), :], AX.X,
                                                  ALU.max, apply_absolute_value=True).then_inc(w_maxed, 1)
                            if next_weights and not more:
                                dve.wait_ge(w_hi, j + 1)
                                dve.scalar_tensor_tensor(out=qkv_lo[:, bass.ds(j, 1), :],
                                                         in0=w_raw[:, bass.ds(j, 1), :], scalar=wsc,
                                                         in1=qkv_hi[:, bass.ds(j, 1), :], op0=ALU.mult,
                                                         op1=ALU.subtract).then_inc(w_lo, 1)
                        chunk(b, NC - 1, 0)
                        if more:
                            for k in range(NK):
                                norm.low(dve, b + 1, k, turn_banks[k])
                        dve.wait_ge(down, b * NC + NC)
                        for i in range(NT):
                            xt = x[:, bass.ds((b * NT + i) * D, D)]
                            dve.tensor_tensor(xt, bank[i][:], xt, ALU.add).then_inc(x_added, 1)

                    batch(0, True, True)
                    if next_weights:
                        dve.wait_ge(w_maxed, NK)
                        weight_scale(dve, NK, c_qkv, w_stat, w_allmax, wsc)
                        dve.tensor_scalar(c_q, c_qkv, HD ** -0.5, None, ALU.mult).then_inc(w_stat, 1)
                        dve.wait_ge(w_stat, 6)
                    with dve.Fori(1, B - 1) as b:
                        batch(b, False, True)
                    batch(B - 1, False, False)

                @block.gpsimd
                def _(pool):
                    norm.invert(pool, 0)
                    norm.invert(pool, 1)
                    if next_weights:
                        pool.wait_ge(w_stat, 1)
                        pool.partition_all_reduce(gmax, rmax, P, RMAX).then_inc(w_allmax, 1)
                    with pool.Fori(2, B) as b:
                        norm.invert(pool, b)

                @block.sync
                def _(sp):
                    for third, loaded in zip(thirds, down_in):
                        cs = slice(third[0], third[-1] + 1)
                        sp.dma_start(w_down[:, cs, :], down_dram[:, cs, :]).then_inc(loaded, 16)
                    if next_weights:
                        sp.wait_ge(dlo, NC)
                        for w, o in next_weights:
                            sp.dma_start(w_raw[:, :, o:o + w.shape[1]], rows(w)).then_inc(w_in, 16)
                    if last_layer:
                        with sp.Fori(0, B) as b:
                            sp.wait_ge(x_added, b * NT + NT)
                            sp.dma_start(out_v[:, bass.ds(b * NT, NT), :], x_v[:, bass.ds(b * NT, NT), :])\
                                .then_inc(stored, 16)
                        sp.wait_ge(stored, 16 * B)
            local.close()
            end_phase()

        qkv_hi = sb("qkv_hi", [P, NK, 3 * D], F16)
        qkv_lo = sb("qkv_lo", [P, NK, 3 * D], F16)
        wo = sb("wo", [P, NK, D], F32)
        prepare()
        phase = ExitStack()
        masks = phase.enter_context(nc.sbuf_tensor("masks", [P, S], F32))
        lnw = phase.enter_context(nc.sbuf_tensor("lnw", [P, 4, D], F32))
        slopes = phase.enter_context(nc.sbuf_tensor("slopes", [P, H], F32))
        attention(False, a["Wout_t"], masks, lnw, slopes, None,
                  [(lnw[:, 0, :], a["q_ln_w"], HD ** -0.5), (lnw[:, 1, :], a["k_ln_w"], 1.0),
                   (lnw[:, 2, :], a["q_ln_b"], HD ** -0.5), (lnw[:, 3, :], a["k_ln_b"], 1.0),
                   (slopes[:], a["alibi_slopes"], 1.0)])
        phase.close()
        ffn(False, [(a["Wq_t"], 0), (a["Wk_t"], D), (a["Wv_t"], 2 * D)])
        phase = ExitStack()
        masks = phase.enter_context(nc.sbuf_tensor("masks_b", [P, S], F32))
        biases = phase.enter_context(nc.sbuf_tensor("biases", [P, 3, D], F32))
        bias_out = phase.enter_context(nc.sbuf_tensor("bias_out", [P, D], F32))
        attention(True, a["Wo_t"], masks, biases, None, bias_out,
                  [(biases[:, 0, :], a["bq"], HD ** -0.5), (biases[:, 1, :], a["bk"], 1.0),
                   (biases[:, 2, :], a["bv"], 1.0), (bias_out[:], a["bo"], 1.0)])
        phase.close()
        ffn(True)


def kernel(**inputs):
    import numpy as np
    import concourse.bacc as bacc
    from concourse.bass_utils import run_bass_kernel_spmd

    def get(name):
        return np.asarray(inputs[name])

    def turned(name):
        return np.ascontiguousarray(get(name).T)

    x = get("L0_attn_a_hidden_states")
    arrays = {
        "x": np.ascontiguousarray(x.reshape(-1, x.shape[-1])),
        "Wqkv_t": turned("L0_attn_a_Wqkv"),
        "Wout_t": turned("L0_attn_a_Wout"),
        "Wq_t": turned("L0_attn_b_Wq"),
        "Wk_t": turned("L0_attn_b_Wk"),
        "Wv_t": turned("L0_attn_b_Wv"),
        "Wo_t": turned("L0_attn_b_Wo"),
        "gate_q_t": turned("L0_ffn_gate_q"),
        "up_q_t": turned("L0_ffn_up_q"),
        "down_q_t": turned("L0_ffn_down_q"),
        "gate_A_t": turned("L0_ffn_gate_A"),
        "up_A_t": turned("L0_ffn_up_A"),
        "down_A_t": turned("L0_ffn_down_A"),
    }
    for name in ("q_ln_w", "q_ln_b", "k_ln_w", "k_ln_b"):
        arrays[name] = get(f"L0_attn_a_{name}")
    for name in ("bq", "bk", "bv", "bo"):
        arrays[name] = get(f"L0_attn_b_{name}")
    for name in ("gate_scale", "gate_B", "up_scale", "up_B", "down_scale", "down_B"):
        arrays[name] = get(f"L0_ffn_{name}")
    arrays["alibi_slopes"] = (1.0 / np.power(2.0, np.arange(1, H + 1, dtype=np.float32) * np.float32(8.0 / H)))\
        .astype(np.float32)

    nc = bacc.Bacc("TRN2", target_bir_lowering=False, num_devices=1)
    args = {name: nc.dram_tensor(f"in_{name}", v.shape, mybir.dt.from_np(v.dtype), kind="ExternalInput").ap()
            for name, v in arrays.items()}
    out = nc.dram_tensor("out_0", (B * S, D), F32, kind="ExternalOutput").ap()
    program(nc, args, out)
    r = run_bass_kernel_spmd(nc, [{f"in_{n}": v for n, v in arrays.items()}], core_ids=[0])
    return r.results[0]["out_0"].reshape(x.shape)
```
